# Optimizing a Trainium2 kernel written in Bass

```python
import numpy as np
import jax
import jax.numpy as jnp

def _softmax(x, axis=-1):
    return jax.nn.softmax(x, axis=axis)

def _gelu(x):
    return jax.nn.gelu(x, approximate=True)

def _silu(x):
    return jax.nn.silu(x)

def _sigmoid(x):
    return jax.nn.sigmoid(x)

def _layernorm(x, axis=-1, eps=1e-05):
    m = jnp.mean(x, axis=axis, keepdims=True)
    v = jnp.var(x, axis=axis, keepdims=True)
    return (x - m) / jnp.sqrt(v + eps)

def _scatter_add(tgt, idx, src, axis=0):
    return tgt.at[idx].add(src)

def _segment_sum(src, seg, n):
    return jax.ops.segment_sum(src, seg, n)
kernel_name = 'mk_seq_postln_d1_jaxref_r4_4a9640'

def setup_inputs(seed: int=0):
    np.random.seed(seed)
    _w = jnp.asarray

    def _L0_attn_setup():
        import jax, jax.numpy as jnp
        import numpy as np
        EPS = 1e-12
        key = jax.random.key(seed)
        k1, k2 = jax.random.split(key)
        b, n, d = (4, 1024, 256)
        x = jax.random.normal(k1, (b, n, d), dtype=jnp.float32)
        W_qkva = jax.random.normal(k2, (3 * d, d), dtype=jnp.float32) * 0.02
        gamma = jnp.ones((d,), dtype=jnp.float32)
        return {'x': x, 'W_qkva': W_qkva, 'gamma': gamma}
    _L0_attn_in = _L0_attn_setup()

    def _L0_ffn_setup():
        import jax, jax.numpy as jnp
        import numpy as np
        DIM = 256
        HIDDEN = 768
        SCALE = 1.0 / 127.0

        def _dequant(w_int, dtype):
            return w_int.astype(dtype) * jnp.asarray(SCALE, dtype)
        key = jax.random.key(seed)
        k_x, k_g, k_u, k_d = jax.random.split(key, 4)
        x = jax.random.normal(k_x, (4, 512, DIM), dtype=jnp.float32)
        w_gate = jax.random.randint(k_g, (HIDDEN, DIM), -127, 128, dtype=jnp.int32)
        w_up = jax.random.randint(k_u, (HIDDEN, DIM), -127, 128, dtype=jnp.int32)
        w_down = jax.random.randint(k_d, (DIM, HIDDEN), -127, 128, dtype=jnp.int32)
        return {'x': x, 'w_gate': w_gate, 'w_up': w_up, 'w_down': w_down}
    _L0_ffn_in = _L0_ffn_setup()
    _d = {'L0_attn_x': _L0_attn_in['x'], 'L0_attn_W_qkva': _L0_attn_in['W_qkva'], 'L0_attn_gamma': _L0_attn_in['gamma'], 'L0_ffn_w_gate': _L0_ffn_in['w_gate'], 'L0_ffn_w_up': _L0_ffn_in['w_up'], 'L0_ffn_w_down': _L0_ffn_in['w_down']}
    _x0 = _d['L0_attn_x']
    _d['L0_attn_x'] = jax.random.normal(jax.random.fold_in(jax.random.key(seed), 1), (16, 512, 256), dtype=_x0.dtype)
    del _x0
    return _d

def reference(L0_attn_x, L0_attn_W_qkva, L0_attn_gamma, L0_ffn_w_gate, L0_ffn_w_up, L0_ffn_w_down):

    def _L0_attn_ref(x, W_qkva, gamma):
        import jax, jax.numpy as jnp
        import numpy as np
        EPS = 1e-12
        d = gamma.shape[0]
        scale = d ** 0.5
        norm = jnp.maximum(jnp.linalg.norm(x, axis=-1, keepdims=True), EPS)
        xn = x / norm * scale * gamma
        h = jnp.einsum('bnd,ed->bne', xn, W_qkva)
        q, kv, a = jnp.split(h, 3, axis=-1)
        a = jax.nn.sigmoid(a)

        def binop(e_i, e_j):
            a_i, kv_i = e_i
            a_j, kv_j = e_j
            return (a_j * a_i, a_j * kv_i + kv_j)
        _, y = jax.lax.associative_scan(binop, (a, kv), axis=1)
        return q * y

    def _L0_ffn_ref(x, w_gate, w_up, w_down):
        import jax, jax.numpy as jnp
        import numpy as np
        DIM = 256
        HIDDEN = 768
        SCALE = 1.0 / 127.0

        def _dequant(w_int, dtype):
            return w_int.astype(dtype) * jnp.asarray(SCALE, dtype)
        wg = _dequant(w_gate, x.dtype)
        wu = _dequant(w_up, x.dtype)
        wd = _dequant(w_down, x.dtype)
        gate = jnp.einsum('bsd,hd->bsh', x, wg)
        up = jnp.einsum('bsd,hd->bsh', x, wu)
        h = jax.nn.silu(gate) * up
        return jnp.einsum('bsh,dh->bsd', h, wd)
    x = L0_attn_x
    x = _layernorm(x + _L0_attn_ref(x, L0_attn_W_qkva, L0_attn_gamma), axis=-1)
    x = _layernorm(x + _L0_ffn_ref(x, L0_ffn_w_gate, L0_ffn_w_up, L0_ffn_w_down), axis=-1)
    return x

_drawn_inputs = setup_inputs


def setup_inputs(seed=0):
    import zlib

    import numpy as np

    out = dict(_drawn_inputs(seed))
    spreads = {'L0_attn_gamma': (1.0, 0.2)}
    factors = {}
    for name, (base, spread) in spreads.items():
        noise = np.random.default_rng([zlib.crc32(name.encode()), seed]).standard_normal(out[name].shape)
        drawn = base * np.exp(spread * noise) if base else spread * noise
        out[name] = jnp.asarray(drawn.astype(out[name].dtype))
    for name, factor in factors.items():
        out[name] = (out[name] * factor).astype(out[name].dtype)
    return out
```

```python
import concourse.bass as bass
from concourse import mybir
from contextlib import ExitStack


def post_norm_scan_ffn(nc, x_nat, x_fm, w_qkva, gamma, w_gate, w_up, w_down, out):
    fp32, fp32r, i32 = mybir.dt.float32, mybir.dt.float32r, mybir.dt.int32
    ALU, ACT = mybir.AluOpType, mybir.ActivationFunctionType

    P = 128
    NB, _, TT, D = x_nat.shape
    N = TT * P
    C = D // P
    E = w_qkva.shape[2]
    H = w_gate.shape[2]
    HC = H // P
    DEQUANT = 1.0 / 127.0
    LN_EPS = 1e-5
    NORM_EPS = 1e-12
    ROOT_D = float(D) ** 0.5

    Q, KV, A = 0, 1, 2
    PROJ = [(A, 0), (KV, 0), (Q, 0), (A, 1), (KV, 1), (Q, 1)]
    NPROJ = len(PROJ)
    A_AT, KV_AT, Q_AT = [0, 3], [1, 4], [2, 5]
    R_BANK = 2
    RN_BANK = 4
    DOWN_BANK = 4
    X1_BANK = 6
    GU_BANK = [6, 0]

    FIRST, LAST = -2, NB
    LOOP = range(1, NB - 3, 2)

    def has_proj(s):
        return s is None or 0 <= s + 1 < NB

    def has_ffn(s):
        return s is None or 0 <= s < NB

    def has_norm(s):
        return s is None or 0 <= s + 2 < NB

    def has_final(s):
        return s is None or 0 <= s - 1 < NB

    def has_load(s):
        return s is None or 0 <= s + 3 < NB

    def run_steps(eng, step, first=FIRST):
        for s in range(first, LOOP.start):
            step(s, s, s % 2)
        with eng.Fori(LOOP.start, LOOP[-1] + 1, LOOP.step) as s:
            for k in range(LOOP.step):
                step(s + k, None, (LOOP.start + k) % 2)
        for s in range(LOOP[-1] + LOOP.step, LAST + 1):
            step(s, s, s % 2)

    ctx = ExitStack()
    with ctx:
        def sb(name, shape, dt=fp32):
            return ctx.enter_context(nc.sbuf_tensor(name, shape, dt))

        def sem(name):
            return ctx.enter_context(nc.semaphore(name))

        qkva_raw = sb("qkva_raw", [P, C, E])
        gamma_sb = sb("gamma_sb", [P, C])
        qkva_sc = sb("qkva_sc", [P, C, E])
        qkva_hi, qkva_lo = sb("qkva_hi", [P, C, E], fp32r), sb("qkva_lo", [P, C, E], fp32r)
        gate_i, up_i = sb("gate_i", [P, C, H], i32), sb("up_i", [P, C, H], i32)
        down_i = sb("down_i", [P, HC, D], i32)
        gate_hi, gate_lo = sb("gate_hi", [P, C, H], fp32r), sb("gate_lo", [P, C, H], fp32r)
        up_hi, up_lo = sb("up_hi", [P, C, H], fp32r), sb("up_lo", [P, C, H], fp32r)
        down_hi, down_lo = sb("down_hi", [P, HC, D], fp32r), sb("down_lo", [P, HC, D], fp32r)
        lo_sums = sb("lo_sums", [P, 3])
        lo_any = sb("lo_any", [P, 1])
        lo_flag = sb("lo_flag", [1, 1], i32)
        ident = sb("ident", [P, P])
        ones = sb("ones", [P, 1])
        minus_half = sb("minus_half", [P, TT])
        xn_in = sb("xn_in", [P, TT, D])
        xf_in = sb("xf_in", [P, 2, C, N])
        squares = sb("squares", [P, TT, D])
        sum_sq = sb("sum_sq", [P, TT])
        sum_sq_floor = sb("sum_sq_floor", [P, TT])
        inv_norm = sb("inv_norm", [P, TT])
        xn = sb("xn", [P, C, N])
        xn_hi, xn_lo = sb("xn_hi", [P, C, N], fp32r), sb("xn_lo", [P, C, N], fp32r)
        tanh_a = sb("tanh_a", [P, C, N])
        decay = sb("decay", [P, C, N])
        y = sb("y", [P, C, N])
        qy = sb("qy", [P, C, N])
        r_fm = sb("r_fm", [P, C, N])
        stats1, mv1 = sb("stats1", [P, TT, 6]), sb("mv1", [P, TT, 2])
        var1, rstd1 = sb("var1", [P, TT]), sb("rstd1", [P, TT])
        x1 = sb("x1", [P, 2, TT, D])
        x1_hi, x1_lo = sb("x1_hi", [P, C, N], fp32r), sb("x1_lo", [P, C, N], fp32r)
        silu_g = sb("silu_g", [P, 2, N])
        h = sb("h", [P, 2, N])
        h_hi, h_lo = sb("h_hi", [P, HC, N], fp32r), sb("h_lo", [P, HC, N], fp32r)
        r2 = sb("r2", [P, TT, D])
        stats2, mv2 = sb("stats2", [P, TT, 6]), sb("mv2", [P, TT, 2])
        var2, rstd2 = sb("var2", [P, TT]), sb("rstd2", [P, TT])
        out_sb = sb("out_sb", [P, TT, D])

        ps = ctx.enter_context(nc.psum_tensor("ps", [P, 8, N], fp32))

        s_xn_in = sem("s_xn_in")
        s_xf_in = [sem("s_xf_in0"), sem("s_xf_in1")]
        s_w_qkva, s_gamma = sem("s_w_qkva"), sem("s_gamma")
        s_w_gate, s_w_up, s_w_down = sem("s_w_gate"), sem("s_w_up"), sem("s_w_down")
        s_stored = sem("s_stored")
        s_ident0, s_ident, s_const = sem("s_ident0"), sem("s_ident"), sem("s_const")
        s_qkva_sc, s_qkva_hi, s_qkva_lo = sem("s_qkva_sc"), sem("s_qkva_hi"), sem("s_qkva_lo")
        s_int_hi, s_int_lo = sem("s_int_hi"), sem("s_int_lo")
        s_lo_sums, s_lo_any0, s_lo_any = sem("s_lo_sums"), sem("s_lo_any0"), sem("s_lo_any")
        s_lo_count, s_lo_flag = sem("s_lo_count"), sem("s_lo_flag")
        s_sum_sq, s_floor, s_inv_norm = sem("s_sum_sq"), sem("s_floor"), sem("s_inv_norm")
        s_rn, s_xn, s_xn_hi, s_xn_lo = sem("s_rn"), sem("s_xn"), sem("s_xn_hi"), sem("s_xn_lo")
        s_proj = sem("s_proj")
        s_tanh, s_decay, s_y, s_qy, s_r_fm = (sem(f"s_{n}") for n in ("tanh", "decay", "y", "qy", "r_fm"))
        s_r = sem("s_r")
        s_stats1, s_mv1, s_var1, s_rstd1 = (sem(f"s_{n}") for n in ("stats1", "mv1", "var1", "rstd1"))
        s_x1 = sem("s_x1")
        s_x1_fm, s_x1_hi, s_x1_lo = sem("s_x1_fm"), sem("s_x1_hi"), sem("s_x1_lo")
        s_gu = sem("s_gu")
        s_silu, s_h, s_h_hi, s_h_lo = sem("s_silu"), sem("s_h"), sem("s_h_hi"), sem("s_h_lo")
        s_down, s_r2 = sem("s_down"), sem("s_r2")
        s_stats2, s_mv2, s_var2, s_rstd2 = (sem(f"s_{n}") for n in ("stats2", "mv2", "var2", "rstd2"))
        s_out = sem("s_out")

        def wide(ap):
            return ap.bitcast(fp32)

        block = ctx.enter_context(nc.Block())

        @block.sync
        def _(sp):
            sp.dma_start(xn_in[:, :, :], x_nat[0]).then_inc(s_xn_in, 16)
            sp.dma_start(xf_in[:, 0, :, :], x_fm[0]).then_inc(s_xf_in[0], 16)
            sp.dma_start(qkva_raw[:, :, :], w_qkva).then_inc(s_w_qkva, 16)
            sp.dma_start(xf_in[:, 1, :, :], x_fm[1]).then_inc(s_xf_in[1], 16)

            def step(s, known, parity):
                if has_load(known):
                    sp.wait_ge(s_sum_sq, s + 3)
                    sp.dma_start(xn_in[:, :, :], x_nat[s + 3]).then_inc(s_xn_in, 16)
                if has_final(known):
                    sp.wait_ge(s_out, s)
                    sp.dma_start(out[s - 1], out_sb[:, :, :]).then_inc(s_stored, 16)
                if has_load(known) and known != FIRST:
                    sp.wait_ge(s_r_fm, C * (s + 2))
                    sp.dma_start(xf_in[:, (parity + 3) % 2, :, :], x_fm[s + 3])\
                        .then_inc(s_xf_in[(parity + 3) % 2], 16)

            run_steps(sp, step)
            sp.wait_ge(s_stored, 16 * NB)

        @block.tensor
        def _(pe):
            def proj(s, known):
                pe.wait_ge(s_xn_hi, s + 2)
                pe.wait_ge(s_xn_lo, s + 2)
                if known == -1:
                    pe.wait_ge(s_qkva_hi, C)
                    pe.wait_ge(s_qkva_lo, C)
                for n, (part, c) in enumerate(PROJ):
                    if n == DOWN_BANK and has_final(known):
                        pe.wait_ge(s_r2, 2 * s - 1)
                    if n == DOWN_BANK + 1 and has_final(known):
                        pe.wait_ge(s_r2, 2 * s)
                    e = part * D + c * P
                    passes = [(w, x_, k) for k in range(C)
                              for w, x_ in ((qkva_hi, xn_hi), (qkva_hi, xn_lo), (qkva_lo, xn_hi))]
                    for m, (w, x_, k) in enumerate(passes):
                        last = nc.tensor.matmul(ps[:, n, :], w[:, k, e:e + P], x_[:, k, :],
                                                start=(m == 0), stop=(m == len(passes) - 1))
                    last.then_inc(s_proj, 1)

            def r_to_nat(s):
                pe.wait_ge(s_r_fm, C * (s + 2))
                for t in range(TT):
                    for c in range(C):
                        o = (t % 2) * D + c * P
                        last = nc.tensor.transpose(ps[:, R_BANK + t // 2, o:o + P],
                                                   r_fm[:, c, t * P:(t + 1) * P], ident[:, :])
                    if t % 2:
                        last.then_inc(s_r, 1)

            def spread_norms(s, known):
                pe.wait_ge(s_inv_norm, s + 3)
                if known == FIRST:
                    pe.wait_ge(s_ident, 1)
                for t in range(TT):
                    last = nc.tensor.transpose(ps[:, RN_BANK, t * P:(t + 1) * P],
                                               inv_norm[:, t:t + 1].to_broadcast([P, P]), ident[:, :])
                last.then_inc(s_rn, 1)

            def x1_to_fm(s, known):
                pe.wait_ge(s_x1, TT * (s + 2))
                if has_ffn(known):
                    pe.wait_ge(s_h, HC * s + HC - 1)
                for c in range(C):
                    for t in range(TT):
                        src = x1_src[:, t, c * P:(c + 1) * P]
                        last = nc.tensor.transpose(ps[:, X1_BANK + c, t * P:(t + 1) * P], src, ident[:, :])
                    last.then_inc(s_x1_fm, 1)

            def gate_up(s, known, p, general):
                if p == 0:
                    pe.wait_ge(s_x1_hi, C * (s + 1))
                    pe.wait_ge(s_x1_lo, C * (s + 1))
                if p == 1 and has_proj(known):
                    pe.wait_ge(s_y, C * (s + 1) + 1)
                if p >= 2:
                    pe.wait_ge(s_h, HC * s + p - 1)
                for n, (hi, lo) in enumerate(((gate_hi, gate_lo), (up_hi, up_lo))):
                    passes = [(w, x_, k) for w in ((hi, lo) if general else (hi,))
                              for k in range(C) for x_ in (x1_hi, x1_lo)]
                    for m, (w, x_, k) in enumerate(passes):
                        last = nc.tensor.matmul(ps[:, GU_BANK[p % 2] + n, :], w[:, k, p * P:(p + 1) * P],
                                                x_[:, k, :], start=(m == 0), stop=(m == len(passes) - 1))
                    last.then_inc(s_gu, 1)

            def down(s, known, general):
                if has_norm(known):
                    pe.wait_ge(s_xn, s + 3)
                for k in range(HC):
                    pe.wait_ge(s_h_hi, HC * s + k + 1)
                    pe.wait_ge(s_h_lo, HC * s + k + 1)
                    for t in range(TT):
                        o = (t % 2) * D
                        passes = [(h_, w) for w in ((down_hi, down_lo) if general else (down_hi,))
                                  for h_ in (h_hi, h_lo)]
                        for m, (h_, w) in enumerate(passes):
                            last = nc.tensor.matmul(
                                ps[:, DOWN_BANK + t // 2, o:o + D], h_[:, k, t * P:(t + 1) * P], w[:, k, :],
                                start=(k == 0 and t % 2 == 0 and m == 0),
                                stop=(k == HC - 1 and m == len(passes) - 1), skip_group_check=True)
                        if k == HC - 1 and t % 2:
                            last.then_inc(s_down, 1)

            def steps(first, general):
                def step(s, known, parity):
                    nonlocal x1_src
                    x1_src = x1[:, (parity + 1) % 2, :, :]
                    if has_proj(known) and known != 0:
                        proj(s, known)
                    if has_ffn(known):
                        gate_up(s, known, 0, general)
                        gate_up(s, known, 1, general)
                    if has_proj(known):
                        r_to_nat(s)
                    if has_ffn(known):
                        gate_up(s, known, 2, general)
                        gate_up(s, known, 3, general)
                    if has_norm(known):
                        spread_norms(s, known)
                    if has_ffn(known):
                        gate_up(s, known, 4, general)
                        gate_up(s, known, 5, general)
                    if has_proj(known):
                        x1_to_fm(s, known)
                    if has_ffn(known):
                        down(s, known, general)
                return step

            x1_src = None
            for s in range(FIRST, 0):
                steps(FIRST, False)(s, s, s % 2)
            proj(0, 0)
            pe.wait_ge(s_lo_any, 1)
            pe.wait_ge(s_const, 1)
            pe.wait_ge(s_x1_hi, C)
            pe.wait_ge(s_x1_lo, C)
            nc.tensor.matmul(ps[0:1, X1_BANK, 0:1], lo_any[:, :], ones[:, :],
                             start=True, stop=True).then_inc(s_lo_count, 1)
            pe.wait_ge(s_lo_flag, 1)
            flag = pe.value_load(lo_flag[0:1, 0:1], min_val=0, max_val=1)
            with pe.If(flag == 0):
                run_steps(pe, steps(0, False), 0)
            with pe.Else():
                run_steps(pe, steps(0, True), 0)

        @block.scalar
        def _(act):
            act.dma_start(gamma_sb[:, :], gamma).then_inc(s_gamma, 16)
            act.dma_start(gate_i[:, :, :], w_gate).then_inc(s_w_gate, 16)
            act.dma_start(up_i[:, :, :], w_up).then_inc(s_w_up, 16)
            act.dma_start(down_i[:, :, :], w_down).then_inc(s_w_down, 16)

            def tanh(s, c):
                act.wait_ge(s_proj, NPROJ * (s + 1) + A_AT[c] + 1)
                nc.scalar.activation(tanh_a[:, c, :], ps[:, A_AT[c], :], ACT.Tanh, scale=0.5).then_inc(s_tanh, 1)

            def sum_squares(s):
                act.wait_ge(s_xn_in, 16 * (s + 3))
                for t in range(TT):
                    last = nc.scalar.activation(squares[:, t, :], xn_in[:, t, :], ACT.Square,
                                                accum_out=sum_sq[:, t:t + 1])
                last.then_inc(s_sum_sq, 1)

            def split_xn(s):
                act.wait_ge(s_xn, s + 3)
                nc.scalar.activation(xn_hi[:, :, :], xn[:, :, :], ACT.Copy).then_inc(s_xn_hi, 1)

            def silu(s, p):
                act.wait_ge(s_gu, 2 * HC * s + 2 * p + 1)
                nc.scalar.activation(silu_g[:, p % 2, :], ps[:, GU_BANK[p % 2], :], ACT.Silu,
                                     scale=DEQUANT).then_inc(s_silu, 1)

            def split_h(s, p):
                act.wait_ge(s_h, HC * s + p + 1)
                nc.scalar.activation(h_hi[:, p, :], h[:, p % 2, :], ACT.Copy).then_inc(s_h_hi, 1)

            def split_x1(s, c):
                act.wait_ge(s_x1_fm, C * (s + 1) + c + 1)
                nc.scalar.activation(x1_hi[:, c, :], ps[:, X1_BANK + c, :], ACT.Copy).then_inc(s_x1_hi, 1)

            def step(s, known, parity):
                if has_proj(known):
                    tanh(s, 0)
                if has_norm(known):
                    sum_squares(s)
                if known == FIRST:
                    for c in range(C):
                        act.wait_ge(s_qkva_sc, c + 1)
                        nc.scalar.activation(qkva_hi[:, c, :], qkva_sc[:, c, :], ACT.Copy).then_inc(s_qkva_hi, 1)
                if has_proj(known):
                    tanh(s, 1)
                if has_ffn(known):
                    silu(s, 0)
                    for p in range(1, HC - 1):
                        silu(s, p)
                        split_h(s, p - 1)
                if has_norm(known):
                    split_xn(s)
                if has_ffn(known):
                    silu(s, HC - 1)
                    split_h(s, HC - 2)
                    split_h(s, HC - 1)
                if has_proj(known):
                    for c in range(C):
                        split_x1(s, c)
                if known == FIRST:
                    for hi, raw, loaded in ((gate_hi, gate_i, s_w_gate), (up_hi, up_i, s_w_up),
                                            (down_hi, down_i, s_w_down)):
                        act.wait_ge(loaded, 16)
                        nc.scalar.activation(hi[:, :, :], raw[:, :, :], ACT.Copy).then_inc(s_int_hi, 1)
                if known == FIRST + 1:
                    for n, (lo, raw) in enumerate(((gate_lo, gate_i), (up_lo, up_i), (down_lo, down_i))):
                        act.wait_ge(s_int_lo, n + 1)
                        last = nc.scalar.activation(wide(raw[:, :, :]), wide(lo[:, :, :]), ACT.Square,
                                                    accum_out=lo_sums[:, n:n + 1])
                    last.then_inc(s_lo_sums, 1)

            run_steps(act, step)

        @block.vector
        def _(dve):
            def row_stats(n, rows, s_rows, stats, s_stats, mv, s_mv, var, s_var):
                for t in range(TT):
                    if t % 2 == 0:
                        dve.wait_ge(s_rows, 2 * (n - 1) + t // 2 + 1)
                    if t == 2:
                        dve.wait_ge(s_stats, TT * (n - 1) + 2)
                    nc.vector.bn_stats(stats[:, t, :], rows(t)).then_inc(s_stats, 1)
                    if t == 2:
                        nc.vector.bn_aggr(mv[:, 0, :], stats[:, 0, :])
                        nc.vector.bn_aggr(mv[:, 1, :], stats[:, 1, :]).then_inc(s_mv, 1)
                dve.wait_ge(s_stats, TT * n)
                dve.wait_ge(s_mv, 2 * n - 1)
                nc.vector.tensor_scalar_add(var[:, 0:2], mv[:, 0:2, 1], LN_EPS)
                nc.vector.bn_aggr(mv[:, 2, :], stats[:, 2, :])
                nc.vector.bn_aggr(mv[:, 3, :], stats[:, 3, :]).then_inc(s_mv, 1)
                dve.wait_ge(s_mv, 2 * n)
                nc.vector.tensor_scalar_add(var[:, 2:4], mv[:, 2:4, 1], LN_EPS).then_inc(s_var, 1)

            def residual2(s, parity):
                for k in range(2):
                    dve.wait_ge(s_down, 2 * s - 1 + k)
                    nc.vector.scalar_tensor_tensor(
                        out=r2[:, 2 * k:2 * k + 2, :].rearrange("p t d -> p (t d)"), in0=ps[:, DOWN_BANK + k, :],
                        scalar=DEQUANT, op0=ALU.mult,
                        in1=x1[:, (parity + 1) % 2, 2 * k:2 * k + 2, :].rearrange("p t d -> p (t d)"),
                        op1=ALU.add).then_inc(s_r2, 1)
                row_stats(s, lambda t: r2[:, t, :], s_r2, stats2, s_stats2, mv2, s_mv2, var2, s_var2)

            def normalise2(s):
                dve.wait_ge(s_rstd2, s)
                if not isinstance(s, int) or s >= 2:
                    dve.wait_ge(s_stored, 16 * (s - 1))
                for t in range(TT):
                    last = nc.vector.tensor_scalar(out_sb[:, t, :], r2[:, t, :], mv2[:, t, 0:1], rstd2[:, t:t + 1],
                                                   ALU.subtract, ALU.mult)
                last.then_inc(s_out, 1)

            def attention(s, c):
                n = C * (s + 1) + c + 1
                dve.wait_ge(s_tanh, n)
                nc.vector.tensor_scalar(decay[:, c, :], tanh_a[:, c, :], 0.5, 0.5, ALU.mult, ALU.add)\
                    .then_inc(s_decay, 1)
                dve.wait_ge(s_proj, NPROJ * (s + 1) + KV_AT[c] + 1)
                dve.wait_ge(s_decay, n)
                nc.vector.tensor_tensor_scan(out=y[:, c, :], data0=decay[:, c, :], data1=ps[:, KV_AT[c], :],
                                             initial=0.0, op0=ALU.mult, op1=ALU.add).then_inc(s_y, 1)
                dve.wait_ge(s_proj, NPROJ * (s + 1) + Q_AT[c] + 1)
                dve.wait_ge(s_y, n)
                nc.vector.tensor_tensor(out=qy[:, c, :], in0=ps[:, Q_AT[c], :], in1=y[:, c, :], op=ALU.mult)\
                    .then_inc(s_qy, 1)

            def stats_r(s):
                row_stats(s + 2, lambda t: ps[:, R_BANK + t // 2, (t % 2) * D:(t % 2 + 1) * D], s_r,
                          stats1, s_stats1, mv1, s_mv1, var1, s_var1)

            def normalise1(s, parity):
                dve.wait_ge(s_rstd1, s + 2)
                for t in range(TT):
                    nc.vector.tensor_scalar(x1[:, (parity + 1) % 2, t, :],
                                            ps[:, R_BANK + t // 2, (t % 2) * D:(t % 2 + 1) * D],
                                            mv1[:, t, 0:1], rstd1[:, t:t + 1],
                                            ALU.subtract, ALU.mult).then_inc(s_x1, 1)

            def hidden(s, p):
                dve.wait_ge(s_gu, 2 * HC * s + 2 * p + 2)
                dve.wait_ge(s_silu, HC * s + p + 1)
                if p >= 2:
                    dve.wait_ge(s_h_hi, HC * s + p - 1)
                    dve.wait_ge(s_h_lo, HC * s + p - 1)
                nc.vector.scalar_tensor_tensor(out=h[:, p % 2, :], in0=ps[:, GU_BANK[p % 2] + 1, :], scalar=DEQUANT,
                                               op0=ALU.mult, in1=silu_g[:, p % 2, :], op1=ALU.mult)\
                    .then_inc(s_h, 1)

            def floor_norm(s):
                dve.wait_ge(s_sum_sq, s + 3)
                nc.vector.tensor_scalar_max(sum_sq_floor[:, :], sum_sq[:, :], NORM_EPS ** 2).then_inc(s_floor, 1)

            def normalise_x(s, parity):
                dve.wait_ge(s_xf_in[parity], 16 * ((s + 2 - parity) // 2 + 1) if isinstance(s, int) else 8 * (s + 4 - parity))
                dve.wait_ge(s_rn, s + 3)
                nc.vector.tensor_tensor(out=xn[:, :, :], in0=xf_in[:, parity, :, :],
                                        in1=ps[:, RN_BANK:RN_BANK + 1, :].to_broadcast([P, C, N]),
                                        op=ALU.mult).then_inc(s_xn, 1)

            def split_x1(s, c):
                dve.wait_ge(s_x1_hi, C * (s + 1) + c + 1)
                nc.vector.tensor_tensor(out=x1_lo[:, c, :], in0=ps[:, X1_BANK + c, :], in1=wide(x1_hi[:, c, :]),
                                        op=ALU.subtract).then_inc(s_x1_lo, 1)

            def split_xn(s):
                dve.wait_ge(s_xn_hi, s + 3)
                nc.vector.tensor_tensor(out=xn_lo[:, :, :], in0=xn[:, :, :], in1=wide(xn_hi[:, :, :]),
                                        op=ALU.subtract).then_inc(s_xn_lo, 1)

            def step(s, known, parity):
                if known == FIRST:
                    dve.wait_ge(s_gamma, 16)
                    dve.wait_ge(s_w_qkva, 16)
                    for c in range(C):
                        nc.vector.tensor_scalar(qkva_sc[:, c, :], qkva_raw[:, c, :], gamma_sb[:, c:c + 1], ROOT_D,
                                                ALU.mult, ALU.mult).then_inc(s_qkva_sc, 1)
                if has_final(known):
                    residual2(s, parity)
                if has_proj(known):
                    attention(s, 0)
                if has_norm(known):
                    floor_norm(s)
                if has_final(known):
                    normalise2(s)
                if has_proj(known):
                    attention(s, 1)
                if has_ffn(known):
                    hidden(s, 0)
                    hidden(s, 1)
                if has_proj(known):
                    stats_r(s)
                if has_ffn(known):
                    hidden(s, 2)
                if has_proj(known):
                    normalise1(s, parity)
                if has_ffn(known):
                    hidden(s, 3)
                if has_norm(known):
                    normalise_x(s, parity)
                if has_ffn(known):
                    hidden(s, 4)
                    hidden(s, 5)
                if has_proj(known):
                    for c in range(C):
                        split_x1(s, c)
                if known == FIRST:
                    for c in range(C):
                        dve.wait_ge(s_qkva_hi, c + 1)
                        nc.vector.tensor_tensor(out=qkva_lo[:, c, :], in0=qkva_sc[:, c, :],
                                                in1=wide(qkva_hi[:, c, :]), op=ALU.subtract).then_inc(s_qkva_lo, 1)
                if has_norm(known):
                    split_xn(s)
                if known == FIRST + 1:
                    for n, (lo, raw, hi) in enumerate(((gate_lo, gate_i, gate_hi), (up_lo, up_i, up_hi),
                                                       (down_lo, down_i, down_hi))):
                        dve.wait_ge(s_int_hi, n + 1)
                        nc.vector.tensor_tensor(out=lo[:, :, :], in0=raw[:, :, :], in1=wide(hi[:, :, :]),
                                                op=ALU.subtract).then_inc(s_int_lo, 1)
                    dve.wait_ge(s_lo_sums, 1)
                    nc.vector.reduce_sum(lo_any[:, :], lo_sums[:, :], mybir.AxisListType.X).then_inc(s_lo_any0, 1)
                    dve.wait_ge(s_lo_any0, 1)
                    nc.vector.tensor_scalar_min(lo_any[:, :], lo_any[:, :], 1.0).then_inc(s_lo_any, 1)
                    dve.wait_ge(s_lo_count, 1)
                    nc.vector.tensor_scalar_min(lo_flag[:, :], ps[0:1, X1_BANK, 0:1], 1.0).then_inc(s_lo_flag, 1)

            run_steps(dve, step)

        @block.gpsimd
        def _(pool):
            pool.memset(ident[:, :], 0.0).then_inc(s_ident0, 1)
            pool.memset(minus_half[:, :], -0.5).then_inc(s_ident0, 1)
            pool.wait_ge(s_ident0, 2)
            pool.affine_select(out=ident[:, :], in_=ident[:, :], compare_op=ALU.not_equal, fill=1.0,
                               base=0, pattern=[[-1, P]], channel_multiplier=1).then_inc(s_ident, 1)
            pool.memset(ones[:, :], 1.0).then_inc(s_const, 1)

            def inverse_std(var, s_var, rstd, s_rstd, n):
                pool.wait_ge(s_var, n)
                nc.gpsimd.tensor_tensor(out=rstd[:, :], in0=var[:, :], in1=minus_half[:, :], op=ALU.pow)\
                    .then_inc(s_rstd, 1)

            def inverse_norm(s):
                pool.wait_ge(s_floor, s + 3)
                nc.gpsimd.tensor_tensor(out=inv_norm[:, :], in0=sum_sq_floor[:, :], in1=minus_half[:, :],
                                        op=ALU.pow).then_inc(s_inv_norm, 1)

            def residual1(s, parity, c):
                pool.wait_ge(s_qy, C * (s + 1) + c + 1)
                nc.gpsimd.tensor_tensor(out=r_fm[:, c, :], in0=qy[:, c, :], in1=xf_in[:, (parity + 1) % 2, c, :],
                                        op=ALU.add).then_inc(s_r_fm, 1)

            def split_h(s, p):
                pool.wait_ge(s_h_hi, HC * s + p + 1)
                nc.gpsimd.tensor_tensor(out=h_lo[:, p, :], in0=h[:, p % 2, :], in1=wide(h_hi[:, p, :]),
                                        op=ALU.subtract).then_inc(s_h_lo, 1)

            def step(s, known, parity):
                if has_final(known):
                    inverse_std(var2, s_var2, rstd2, s_rstd2, s)
                if has_norm(known):
                    inverse_norm(s)
                if has_proj(known):
                    residual1(s, parity, 0)
                    residual1(s, parity, 1)
                if has_ffn(known):
                    split_h(s, 0)
                    split_h(s, 1)
                if has_proj(known):
                    inverse_std(var1, s_var1, rstd1, s_rstd1, s + 2)
                if has_ffn(known):
                    for p in range(2, HC):
                        split_h(s, p)

            run_steps(pool, step)


def kernel(L0_attn_x, L0_attn_W_qkva, L0_attn_gamma, L0_ffn_w_gate, L0_ffn_w_up, L0_ffn_w_down):
    import numpy as np
    import concourse.bacc as bacc
    from concourse.bass_utils import run_bass_kernel_spmd

    P = 128
    x = np.asarray(L0_attn_x)
    nb, n, d = x.shape

    def by_partition(w):
        w = np.asarray(w)
        return np.ascontiguousarray(w.T.reshape(-1, P, w.shape[0]).transpose(1, 0, 2))

    arrays = {
        "x_nat": np.ascontiguousarray(x.reshape(nb, n // P, P, d).transpose(0, 2, 1, 3)),
        "x_fm": np.ascontiguousarray(x.transpose(0, 2, 1).reshape(nb, d // P, P, n).transpose(0, 2, 1, 3)),
        "w_qkva": by_partition(L0_attn_W_qkva),
        "gamma": np.ascontiguousarray(np.asarray(L0_attn_gamma).reshape(d // P, P).T),
        "w_gate": by_partition(L0_ffn_w_gate),
        "w_up": by_partition(L0_ffn_w_up),
        "w_down": by_partition(L0_ffn_w_down),
    }
    nc = bacc.Bacc("TRN2", target_bir_lowering=False, num_devices=1)
    args = [nc.dram_tensor(name, a.shape, mybir.dt.from_np(a.dtype), kind="ExternalInput").ap()
            for name, a in arrays.items()]
    out = nc.dram_tensor("out", arrays["x_nat"].shape, mybir.dt.float32, kind="ExternalOutput").ap()
    post_norm_scan_ffn(nc, *args, out)
    r = run_bass_kernel_spmd(nc, [arrays], core_ids=[0])
    got = np.asarray(r.results[0]["out"])
    return np.ascontiguousarray(got.transpose(0, 2, 1, 3).reshape(nb, n, d))
```

```python
import concourse.bass as bass
from concourse import mybir
from contextlib import ExitStack


def post_norm_scan_ffn(nc, x_rows, x_fm, w_qkva, gamma, w_gate, w_up, w_down, norms_dram, out):
    fp32, fp32r, i32 = mybir.dt.float32, mybir.dt.float32r, mybir.dt.int32
    ALU, ACT = mybir.AluOpType, mybir.ActivationFunctionType

    P = 128
    NB, _, TT, D = x_rows.shape
    N = TT * P
    C = D // P
    E = w_qkva.shape[2]
    H = w_gate.shape[2]
    HC = H // P
    DEQUANT = 1.0 / 127.0
    LN_EPS = 1e-5
    NORM_EPS = 1e-12
    ROOT_D = float(D) ** 0.5

    Q, KV, A = 0, 1, 2
    PROJ = [(A, 0), (KV, 0), (A, 1), (KV, 1), (Q, 0), (Q, 1)]
    NPROJ = len(PROJ)
    A_AT, KV_AT, Q_AT = [0, 2], [1, 3], [4, 5]
    R_BANK = 2
    NORM_BANK = 6
    DOWN_BANK = 4
    X1_BANK = 6
    GU_BANK = [6, 0]

    FIRST, LAST = -2, NB
    LOOP = range(1, NB - 3, 2)

    def has_proj(s):
        return s is None or 0 <= s + 1 < NB

    def has_ffn(s):
        return s is None or 0 <= s < NB

    def has_norm(s):
        return s is None or 0 <= s < NB - 2

    def has_final(s):
        return s is None or 0 <= s - 1 < NB

    def has_load(s):
        return s is None or 2 <= s + 3 < NB

    def run_steps(eng, step, first=FIRST):
        for s in range(first, LOOP.start):
            step(s, s, s % 2)
        with eng.Fori(LOOP.start, LOOP[-1] + 1, LOOP.step) as s:
            for k in range(LOOP.step):
                step(s + k, None, (LOOP.start + k) % 2)
        for s in range(LOOP[-1] + LOOP.step, LAST + 1):
            step(s, s, s % 2)

    ctx = ExitStack()
    with ctx:
        def sb(name, shape, dt=fp32):
            return ctx.enter_context(nc.sbuf_tensor(name, shape, dt))

        def sem(name):
            return ctx.enter_context(nc.semaphore(name))

        qkva_raw = sb("qkva_raw", [P, C, E])
        gamma_sb = sb("gamma_sb", [P, C])
        gamma_root = sb("gamma_root", [P, C])
        qkva_hi, qkva_lo = sb("qkva_hi", [P, C, E], fp32r), sb("qkva_lo", [P, C, E], fp32r)
        gate_i, up_i = sb("gate_i", [P, C, H], i32), sb("up_i", [P, C, H], i32)
        down_i = sb("down_i", [P, HC, D], i32)
        gate_hi, gate_lo = sb("gate_hi", [P, C, H], fp32r), sb("gate_lo", [P, C, H], fp32r)
        up_hi, up_lo = sb("up_hi", [P, C, H], fp32r), sb("up_lo", [P, C, H], fp32r)
        down_hi, down_lo = sb("down_hi", [P, HC, D], fp32r), sb("down_lo", [P, HC, D], fp32r)
        lo_sums = sb("lo_sums", [P, 3])
        lo_any = sb("lo_any", [P, 1])
        lo_flag = sb("lo_flag", [1, 1], i32)
        ident = sb("ident", [P, P])
        ones = sb("ones", [P, 1])
        table_probe = sb("table_probe", [P, 1])
        minus_half = sb("minus_half", [P, TT])
        xn_in = sb("xn_in", [P, 2, TT, D])
        xf_in = sb("xf_in", [P, 2, C, N])
        sum_sq = sb("sum_sq", [P, TT])
        sum_sq_floor = sb("sum_sq_floor", [P, TT])
        inv_norm = sb("inv_norm", [P, TT])
        xn = sb("xn", [P, C, N])
        norm_rows = sb("norm_rows", [P, N])
        xn_hi, xn_lo = sb("xn_hi", [P, 2, C, N], fp32r), sb("xn_lo", [P, 2, C, N], fp32r)
        decay = sb("decay", [P, C, N])
        y = sb("y", [P, C, N])
        qy = sb("qy", [P, C, N])
        r_fm = sb("r_fm", [P, C, N])
        stats1, mv1 = sb("stats1", [P, TT, 6]), sb("mv1", [P, TT, 2])
        var1, rstd1 = sb("var1", [P, TT]), sb("rstd1", [P, TT])
        x1 = sb("x1", [P, 2, TT, D])
        x1_hi, x1_lo = sb("x1_hi", [P, C, N], fp32r), sb("x1_lo", [P, C, N], fp32r)
        silu_g = sb("silu_g", [P, 2, N])
        h = sb("h", [P, 2, N])
        h_hi, h_lo = sb("h_hi", [P, HC, N], fp32r), sb("h_lo", [P, HC, N], fp32r)
        r2 = sb("r2", [P, TT, D])
        stats2, mv2 = sb("stats2", [P, TT, 6]), sb("mv2", [P, TT, 2])
        var2, rstd2 = sb("var2", [P, TT]), sb("rstd2", [P, TT])
        out_sb = sb("out_sb", [P, TT, D])

        ps = ctx.enter_context(nc.psum_tensor("ps", [P, 8, N], fp32))

        s_xn_in = [sem("s_xn_in0"), sem("s_xn_in1")]
        s_xf_in = [sem("s_xf_in0"), sem("s_xf_in1")]
        s_w_qkva, s_gamma = sem("s_w_qkva"), sem("s_gamma")
        s_w_gate, s_w_up, s_w_down = sem("s_w_gate"), sem("s_w_up"), sem("s_w_down")
        s_norms_out, s_norm_rows = sem("s_norms_out"), sem("s_norm_rows")
        s_stored = sem("s_stored")
        s_ident0, s_ident, s_const = sem("s_ident0"), sem("s_ident"), sem("s_const")
        s_gamma_root, s_qkva_hi, s_qkva_lo = sem("s_gamma_root"), sem("s_qkva_hi"), sem("s_qkva_lo")
        s_int_hi, s_int_lo = sem("s_int_hi"), sem("s_int_lo")
        s_lo_sums, s_lo_any0, s_lo_any = sem("s_lo_sums"), sem("s_lo_any0"), sem("s_lo_any")
        s_lo_count, s_lo_flag = sem("s_lo_count"), sem("s_lo_flag")
        s_sum_sq, s_floor, s_inv_norm = sem("s_sum_sq"), sem("s_floor"), sem("s_inv_norm")
        s_first_norms, s_xn, s_xn_hi, s_xn_lo = sem("s_first_norms"), sem("s_xn"), sem("s_xn_hi"), sem("s_xn_lo")
        s_proj = sem("s_proj")
        s_tanh, s_decay, s_y, s_qy, s_r_fm = (sem(f"s_{n}") for n in ("tanh", "decay", "y", "qy", "r_fm"))
        s_r = sem("s_r")
        s_stats1, s_mv1, s_var1, s_rstd1 = (sem(f"s_{n}") for n in ("stats1", "mv1", "var1", "rstd1"))
        s_x1 = sem("s_x1")
        s_x1_fm, s_x1_hi, s_x1_lo = sem("s_x1_fm"), sem("s_x1_hi"), sem("s_x1_lo")
        s_gu = sem("s_gu")
        s_silu, s_h, s_h_hi, s_h_lo = sem("s_silu"), sem("s_h"), sem("s_h_hi"), sem("s_h_lo")
        s_down, s_r2 = sem("s_down"), sem("s_r2")
        s_stats2, s_mv2, s_var2, s_rstd2 = (sem(f"s_{n}") for n in ("stats2", "mv2", "var2", "rstd2"))
        s_out = sem("s_out")

        def wide(ap):
            return ap.bitcast(fp32)

        block = ctx.enter_context(nc.Block())

        @block.sync
        def _(sp):
            norms_flat = norms_dram.rearrange("b p t -> b (p t)")

            def norms_to_rows(b, parity):
                sp.wait_ge(s_inv_norm, b + 1)
                sp.dma_start(norms_dram[parity], inv_norm[:, :]).then_inc(s_norms_out, 16)
                sp.wait_ge(s_norms_out, 16 * (b - 1))
                sp.dma_start(norm_rows[:, :], norms_flat[parity:parity + 1, :].to_broadcast([P, N]))\
                    .then_inc(s_norm_rows, 16)

            sp.dma_start(xn_in[:, 0, :, :], x_rows[0]).then_inc(s_xn_in[0], 16)
            sp.dma_start(qkva_raw[:, :, :], w_qkva).then_inc(s_w_qkva, 16)
            sp.dma_start(xf_in[:, 0, :, :], x_fm[0]).then_inc(s_xf_in[0], 16)
            sp.dma_start(xn_in[:, 1, :, :], x_rows[1]).then_inc(s_xn_in[1], 16)
            sp.dma_start(gate_i[:, :, :], w_gate).then_inc(s_w_gate, 16)
            sp.dma_start(xf_in[:, 1, :, :], x_fm[1]).then_inc(s_xf_in[1], 16)
            sp.dma_start(up_i[:, :, :], w_up).then_inc(s_w_up, 16)
            sp.dma_start(down_i[:, :, :], w_down).then_inc(s_w_down, 16)

            def step(s, known, parity):
                if has_load(known):
                    sp.wait_ge(s_sum_sq, s + 2)
                    sp.dma_start(xn_in[:, (parity + 1) % 2, :, :], x_rows[s + 3])\
                        .then_inc(s_xn_in[(parity + 1) % 2], 16)
                if has_norm(known):
                    norms_to_rows(s + 2, parity)
                if known == NB:
                    for k in range(2):
                        sp.wait_ge(s_out, NB + k)
                        sp.dma_start(out[NB - 1][:, 2 * k:2 * k + 2, :], out_sb[:, 2 * k:2 * k + 2, :])\
                            .then_inc(s_stored, 16)
                elif has_final(known):
                    sp.wait_ge(s_out, s)
                    sp.dma_start(out[s - 1], out_sb[:, :, :]).then_inc(s_stored, 16)
                if has_load(known):
                    sp.wait_ge(s_r_fm, C * (s + 2))
                    sp.dma_start(xf_in[:, (parity + 1) % 2, :, :], x_fm[s + 3])\
                        .then_inc(s_xf_in[(parity + 1) % 2], 16)

            run_steps(sp, step)
            sp.wait_ge(s_stored, 16 * (NB + 1))

        @block.tensor
        def _(pe):
            def proj(s, known, outputs=range(NPROJ)):
                x_parity = (s + 1) % 2 if known is not None else (parity_now + 1) % 2
                batch0_read = [(s_tanh, 1), (s_y, 1), (s_tanh, 2), (s_y, 2), (s_qy, 1), (s_qy, 2)]
                for n in outputs:
                    part, c = PROJ[n]
                    if known == 0:
                        pe.wait_ge(*batch0_read[n])
                    if n == DOWN_BANK and has_final(known):
                        pe.wait_ge(s_r2, 2 * s - 1)
                    if n == DOWN_BANK + 1 and has_final(known):
                        pe.wait_ge(s_r2, 2 * s)
                    e = part * D + c * P
                    for k in range(C):
                        for w, x_ in ((qkva_hi, xn_hi), (qkva_hi, xn_lo), (qkva_lo, xn_hi)):
                            if n == 0 and w is qkva_hi:
                                pe.wait_ge(s_xn_hi if x_ is xn_hi else s_xn_lo, C * (s + 1) + k + 1)
                            if n == 0 and known == -1 and x_ is xn_hi:
                                pe.wait_ge(s_qkva_hi if w is qkva_hi else s_qkva_lo, k + 1)
                            last = nc.tensor.matmul(ps[:, n, :], w[:, k, e:e + P], x_[:, x_parity, k, :],
                                                    start=(k == 0 and w is qkva_hi and x_ is xn_hi),
                                                    stop=(k == C - 1 and w is qkva_lo))
                    last.then_inc(s_proj, 1)

            def r_to_nat(s, bank):
                for c in range(C):
                    pe.wait_ge(s_r_fm, C * (s + 1) + c + 1)
                    for t in range(TT):
                        o = (t % 2) * D + c * P
                        last = nc.tensor.transpose(ps[:, bank + t // 2, o:o + P],
                                                   r_fm[:, c, t * P:(t + 1) * P], ident[:, :])
                        if c == C - 1 and t % 2:
                            last.then_inc(s_r, 1)

            def spread_norms(b):
                pe.wait_ge(s_inv_norm, b + 1)
                pe.wait_ge(s_ident, 1)
                for t in range(TT):
                    last = nc.tensor.transpose(ps[:, NORM_BANK + b, t:N:TT],
                                               inv_norm[:, t:t + 1].to_broadcast([P, P]), ident[:, :])
                last.then_inc(s_first_norms, 1)

            def x1_to_fm(s, known, parity):
                pe.wait_ge(s_x1, TT * (s + 2))
                if has_ffn(known):
                    pe.wait_ge(s_h, HC * s + HC - 1)
                for c in range(C):
                    for t in range(TT):
                        src = x1[:, parity, t, c * P:(c + 1) * P]
                        last = nc.tensor.transpose(ps[:, X1_BANK + c, t * P:(t + 1) * P], src, ident[:, :])
                    last.then_inc(s_x1_fm, 1)

            def gate_up(s, known, p, general):
                if p == 0:
                    pe.wait_ge(s_x1_hi, C * (s + 1))
                    pe.wait_ge(s_x1_lo, C * (s + 1))
                if p == 1 and has_proj(known):
                    pe.wait_ge(s_y, C * (s + 1) + 1)
                if p >= 2:
                    pe.wait_ge(s_h, HC * s + p - 1)
                for n, (hi, lo) in enumerate(((gate_hi, gate_lo), (up_hi, up_lo))):
                    passes = [(w, x_, k) for w in ((hi, lo) if general else (hi,))
                              for k in range(C) for x_ in (x1_hi, x1_lo)]
                    for m, (w, x_, k) in enumerate(passes):
                        last = nc.tensor.matmul(ps[:, GU_BANK[p % 2] + n, :], w[:, k, p * P:(p + 1) * P],
                                                x_[:, k, :], start=(m == 0), stop=(m == len(passes) - 1))
                    last.then_inc(s_gu, 1)

            def down(s, known, general):
                halves = ((0, 1), (2, 3)) if known == NB - 1 else ((0, 1, 2, 3),)
                for tiles in halves:
                    for k in range(HC):
                        if 0 in tiles:
                            pe.wait_ge(s_h_hi, HC * s + k + 1)
                            pe.wait_ge(s_h_lo, HC * s + k + 1)
                        for t in tiles:
                            o = (t % 2) * D
                            passes = [(h_, w) for w in ((down_hi, down_lo) if general else (down_hi,))
                                      for h_ in (h_hi, h_lo)]
                            for m, (h_, w) in enumerate(passes):
                                last = nc.tensor.matmul(
                                    ps[:, DOWN_BANK + t // 2, o:o + D], h_[:, k, t * P:(t + 1) * P], w[:, k, :],
                                    start=(k == 0 and t % 2 == 0 and m == 0),
                                    stop=(k == HC - 1 and m == len(passes) - 1), skip_group_check=True)
                            if k == HC - 1 and t % 2:
                                last.then_inc(s_down, 1)

            def steps(general):
                def step(s, known, parity):
                    nonlocal parity_now
                    parity_now = parity
                    if has_proj(known) and known != 0:
                        proj(s, known)
                    if has_ffn(known):
                        gate_up(s, known, 0, general)
                    if has_proj(known):
                        r_to_nat(s, R_BANK)
                    if has_ffn(known):
                        for p in range(1, HC):
                            gate_up(s, known, p, general)
                    if has_proj(known):
                        x1_to_fm(s, known, (parity + 1) % 2)
                    if has_ffn(known):
                        down(s, known, general)
                return step

            parity_now = 0
            spread_norms(0)
            proj(-1, -1, range(0, 2))
            spread_norms(1)
            proj(-1, -1, range(2, NPROJ))
            proj(0, 0, range(0, 3))
            pe.wait_ge(s_xn, C * 2)
            r_to_nat(-1, X1_BANK)
            proj(0, 0, range(3, NPROJ - 1))
            pe.wait_ge(s_lo_any, 1)
            pe.wait_ge(s_const, 1)
            pe.wait_ge(s_qy, C)
            nc.tensor.matmul(ps[0:1, NPROJ - 1, 0:1], lo_any[:, :], ones[:, :],
                             start=True, stop=True).then_inc(s_lo_count, 1)
            pe.wait_ge(s_lo_flag, 1)
            proj(0, 0, range(NPROJ - 1, NPROJ))
            x1_to_fm(-1, -1, 0)
            flag = pe.value_load(lo_flag[0:1, 0:1], min_val=0, max_val=1)
            with pe.If(flag == 0):
                run_steps(pe, steps(False), 0)
            with pe.Else():
                run_steps(pe, steps(True), 0)

        @block.scalar
        def _(act):
            act.dma_start(gamma_sb[:, :], gamma).then_inc(s_gamma, 16)
            act.wait_ge(s_const, 1)
            nc.scalar.activation(table_probe[:, :], ones[:, :], ACT.Silu)

            def tanh(s, c):
                act.wait_ge(s_proj, NPROJ * (s + 1) + A_AT[c] + 1)
                nc.scalar.activation(decay[:, c, :], ps[:, A_AT[c], :], ACT.Tanh, scale=0.5).then_inc(s_tanh, 1)

            def sum_squares(s, parity):
                act.wait_ge(s_xn_in[parity], 8 * (s + 4 - parity))
                if not isinstance(s, int) or s >= -1:
                    act.wait_ge(s_floor, s + 2)
                for t in range(TT):
                    last = nc.scalar.activation(xn_in[:, parity, t, :], xn_in[:, parity, t, :], ACT.Square,
                                                accum_out=sum_sq[:, t:t + 1])
                last.then_inc(s_sum_sq, 1)

            def split_xn(s, parity):
                for c in range(C):
                    act.wait_ge(s_xn, C * (s + 2) + c + 1)
                    nc.scalar.activation(xn_hi[:, parity, c, :], xn[:, c, :], ACT.Copy).then_inc(s_xn_hi, 1)

            def int_hi(n, hi, raw, loaded):
                act.wait_ge(loaded, 16)
                nc.scalar.activation(hi[:, :, :], raw[:, :, :], ACT.Copy).then_inc(s_int_hi, 1)

            def int_lo_sum(n, lo, raw):
                act.wait_ge(s_int_lo, n + 1)
                nc.scalar.activation(wide(raw[:, :, :]), wide(lo[:, :, :]), ACT.Square,
                                     accum_out=lo_sums[:, n:n + 1]).then_inc(s_lo_sums, 1)

            def silu(s, p):
                act.wait_ge(s_gu, 2 * HC * s + 2 * p + 1)
                nc.scalar.activation(silu_g[:, p % 2, :], ps[:, GU_BANK[p % 2], :], ACT.Silu,
                                     scale=DEQUANT).then_inc(s_silu, 1)

            def split_h(s, p):
                act.wait_ge(s_h, HC * s + p + 1)
                nc.scalar.activation(h_hi[:, p, :], h[:, p % 2, :], ACT.Copy).then_inc(s_h_hi, 1)

            def split_x1(s, c):
                act.wait_ge(s_x1_fm, C * (s + 1) + c + 1)
                nc.scalar.activation(x1_hi[:, c, :], ps[:, X1_BANK + c, :], ACT.Copy).then_inc(s_x1_hi, 1)

            def step(s, known, parity):
                if known == FIRST:
                    sum_squares(FIRST, 0)
                    act.wait_ge(s_w_qkva, 16)
                    act.wait_ge(s_gamma_root, 1)
                    for c in range(C):
                        nc.scalar.activation(qkva_hi[:, c, :], qkva_raw[:, c, :], ACT.Copy,
                                             scale=gamma_root[:, c:c + 1]).then_inc(s_qkva_hi, 1)
                    split_xn(FIRST, 0)
                    sum_squares(FIRST + 1, 1)
                    int_hi(0, gate_hi, gate_i, s_w_gate)
                    split_xn(FIRST + 1, 1)
                if known == FIRST + 1:
                    int_hi(1, up_hi, up_i, s_w_up)
                if has_proj(known):
                    tanh(s, 0)
                if known == FIRST + 1:
                    int_lo_sum(0, gate_lo, gate_i)
                if has_norm(known):
                    sum_squares(s, parity)
                if has_proj(known):
                    tanh(s, 1)
                if known == FIRST + 1:
                    int_hi(2, down_hi, down_i, s_w_down)
                    int_lo_sum(1, up_lo, up_i)
                    int_lo_sum(2, down_lo, down_i)
                if has_ffn(known):
                    silu(s, 0)
                    split_h(s, 0)
                    silu(s, 1)
                    for p in range(2, HC - 1):
                        silu(s, p)
                        split_h(s, p - 1)
                if has_norm(known):
                    split_xn(s, parity)
                if has_ffn(known):
                    silu(s, HC - 1)
                    split_h(s, HC - 2)
                    split_h(s, HC - 1)
                if has_proj(known):
                    for c in range(C):
                        split_x1(s, c)

            run_steps(act, step)

        @block.vector
        def _(dve):
            def row_stats(n, rows, s_rows, stats, s_stats, mv, s_mv, var, s_var):
                for t in range(TT):
                    if t % 2 == 0:
                        dve.wait_ge(s_rows, 2 * (n - 1) + t // 2 + 1)
                    if t == 2:
                        dve.wait_ge(s_stats, TT * (n - 1) + 2)
                    nc.vector.bn_stats(stats[:, t, :], rows(t)).then_inc(s_stats, 1)
                    if t == 2:
                        nc.vector.bn_aggr(mv[:, 0, :], stats[:, 0, :])
                        nc.vector.bn_aggr(mv[:, 1, :], stats[:, 1, :]).then_inc(s_mv, 1)
                dve.wait_ge(s_stats, TT * n)
                dve.wait_ge(s_mv, 2 * n - 1)
                nc.vector.tensor_scalar_add(var[:, 0:2], mv[:, 0:2, 1], LN_EPS)
                nc.vector.bn_aggr(mv[:, 2, :], stats[:, 2, :])
                nc.vector.bn_aggr(mv[:, 3, :], stats[:, 3, :]).then_inc(s_mv, 1)
                dve.wait_ge(s_mv, 2 * n)
                nc.vector.tensor_scalar_add(var[:, 2:4], mv[:, 2:4, 1], LN_EPS).then_inc(s_var, 1)

            def residual2(s, parity):
                for k in range(2):
                    dve.wait_ge(s_down, 2 * s - 1 + k)
                    nc.vector.scalar_tensor_tensor(
                        out=r2[:, 2 * k:2 * k + 2, :].rearrange("p t d -> p (t d)"), in0=ps[:, DOWN_BANK + k, :],
                        scalar=DEQUANT, op0=ALU.mult,
                        in1=x1[:, (parity + 1) % 2, 2 * k:2 * k + 2, :].rearrange("p t d -> p (t d)"),
                        op1=ALU.add).then_inc(s_r2, 1)
                row_stats(s, lambda t: r2[:, t, :], s_r2, stats2, s_stats2, mv2, s_mv2, var2, s_var2)

            def final_half(parity, k):
                tiles = (2 * k, 2 * k + 1)
                dve.wait_ge(s_down, 2 * (NB - 1) + k + 1)
                nc.vector.scalar_tensor_tensor(
                    out=r2[:, 2 * k:2 * k + 2, :].rearrange("p t d -> p (t d)"), in0=ps[:, DOWN_BANK + k, :],
                    scalar=DEQUANT, op0=ALU.mult,
                    in1=x1[:, (parity + 1) % 2, 2 * k:2 * k + 2, :].rearrange("p t d -> p (t d)"),
                    op1=ALU.add).then_inc(s_r2, 1)
                dve.wait_ge(s_r2, 2 * (NB - 1) + k + 1)
                for t in tiles:
                    last = nc.vector.bn_stats(stats2[:, t, :], r2[:, t, :])
                last.then_inc(s_stats2, 1)
                dve.wait_ge(s_stats2, TT * (NB - 1) + k + 1)
                for t in tiles:
                    last = nc.vector.bn_aggr(mv2[:, t, :], stats2[:, t, :])
                last.then_inc(s_mv2, 1)
                dve.wait_ge(s_mv2, 2 * (NB - 1) + k + 1)
                nc.vector.tensor_scalar_add(var2[:, 2 * k:2 * k + 2], mv2[:, 2 * k:2 * k + 2, 1], LN_EPS)\
                    .then_inc(s_var2, 1)
                dve.wait_ge(s_rstd2, NB - 1 + k + 1)
                if k == 0:
                    dve.wait_ge(s_stored, 16 * (NB - 1))
                for t in tiles:
                    last = nc.vector.tensor_scalar(out_sb[:, t, :], r2[:, t, :], mv2[:, t, 0:1], rstd2[:, t:t + 1],
                                                   ALU.subtract, ALU.mult)
                last.then_inc(s_out, 1)

            def normalise2(s):
                dve.wait_ge(s_rstd2, s)
                if not isinstance(s, int) or s >= 2:
                    dve.wait_ge(s_stored, 16 * (s - 1))
                for t in range(TT):
                    last = nc.vector.tensor_scalar(out_sb[:, t, :], r2[:, t, :], mv2[:, t, 0:1], rstd2[:, t:t + 1],
                                                   ALU.subtract, ALU.mult)
                last.then_inc(s_out, 1)

            def scan(s, c):
                n = C * (s + 1) + c + 1
                dve.wait_ge(s_tanh, n)
                nc.vector.tensor_scalar(decay[:, c, :], decay[:, c, :], 0.5, 0.5, ALU.mult, ALU.add)\
                    .then_inc(s_decay, 1)
                dve.wait_ge(s_proj, NPROJ * (s + 1) + KV_AT[c] + 1)
                dve.wait_ge(s_decay, n)
                nc.vector.tensor_tensor_scan(out=y[:, c, :], data0=decay[:, c, :], data1=ps[:, KV_AT[c], :],
                                             initial=0.0, op0=ALU.mult, op1=ALU.add).then_inc(s_y, 1)

            def times_q(s, c):
                dve.wait_ge(s_proj, NPROJ * (s + 1) + Q_AT[c] + 1)
                dve.wait_ge(s_y, C * (s + 1) + c + 1)
                nc.vector.tensor_tensor(out=qy[:, c, :], in0=ps[:, Q_AT[c], :], in1=y[:, c, :], op=ALU.mult)\
                    .then_inc(s_qy, 1)

            def r_rows(known, t):
                bank = (X1_BANK if known == -1 else R_BANK) + t // 2
                return ps[:, bank, (t % 2) * D:(t % 2 + 1) * D]

            def stats_r(s, known):
                row_stats(s + 2, lambda t: r_rows(known, t), s_r,
                          stats1, s_stats1, mv1, s_mv1, var1, s_var1)

            def normalise1(s, known, parity, tiles):
                dve.wait_ge(s_rstd1, s + 2)
                for t in tiles:
                    nc.vector.tensor_scalar(x1[:, (parity + 1) % 2, t, :], r_rows(known, t),
                                            mv1[:, t, 0:1], rstd1[:, t:t + 1],
                                            ALU.subtract, ALU.mult).then_inc(s_x1, 1)

            def hidden(s, p):
                dve.wait_ge(s_gu, 2 * HC * s + 2 * p + 2)
                dve.wait_ge(s_silu, HC * s + p + 1)
                if p >= 2:
                    dve.wait_ge(s_h_hi, HC * s + p - 1)
                    dve.wait_ge(s_h_lo, HC * s + p - 1)
                nc.vector.scalar_tensor_tensor(out=h[:, p % 2, :], in0=ps[:, GU_BANK[p % 2] + 1, :], scalar=DEQUANT,
                                               op0=ALU.mult, in1=silu_g[:, p % 2, :], op1=ALU.mult)\
                    .then_inc(s_h, 1)

            def floor_norm(s):
                dve.wait_ge(s_sum_sq, s + 3)
                nc.vector.tensor_scalar_max(sum_sq_floor[:, :], sum_sq[:, :], NORM_EPS ** 2).then_inc(s_floor, 1)

            def normalise_x(s, parity, c, first=False):
                if c == 0:
                    dve.wait_ge(s_xf_in[parity], 8 * (s + 4 - parity))
                    if first:
                        dve.wait_ge(s_first_norms, s + 3)
                    else:
                        dve.wait_ge(s_norm_rows, 16 * (s + 1))
                norms = ps[:, NORM_BANK + parity, :] if first else norm_rows[:, :]
                nc.vector.tensor_tensor(out=xn[:, c, :], in0=xf_in[:, parity, c, :], in1=norms,
                                        op=ALU.mult).then_inc(s_xn, 1)

            def split_xn(s, parity, chunks=range(C)):
                for c in chunks:
                    dve.wait_ge(s_xn_hi, C * (s + 2) + c + 1)
                    nc.vector.tensor_tensor(out=xn_lo[:, parity, c, :], in0=xn[:, c, :],
                                            in1=wide(xn_hi[:, parity, c, :]), op=ALU.subtract)\
                        .then_inc(s_xn_lo, 1)

            def qkva_lo_part(c):
                dve.wait_ge(s_qkva_hi, c + 1)
                nc.vector.scalar_tensor_tensor(out=qkva_lo[:, c, :], in0=qkva_raw[:, c, :],
                                               scalar=gamma_root[:, c:c + 1], op0=ALU.mult,
                                               in1=wide(qkva_hi[:, c, :]), op1=ALU.subtract)\
                    .then_inc(s_qkva_lo, 1)

            def int_lo(n, lo, raw, hi):
                dve.wait_ge(s_int_hi, n + 1)
                nc.vector.tensor_tensor(out=lo[:, :, :], in0=raw[:, :, :], in1=wide(hi[:, :, :]),
                                        op=ALU.subtract).then_inc(s_int_lo, 1)

            def split_x1(s, c):
                dve.wait_ge(s_x1_hi, C * (s + 1) + c + 1)
                nc.vector.tensor_tensor(out=x1_lo[:, c, :], in0=ps[:, X1_BANK + c, :], in1=wide(x1_hi[:, c, :]),
                                        op=ALU.subtract).then_inc(s_x1_lo, 1)

            def step(s, known, parity):
                if known == FIRST:
                    dve.wait_ge(s_gamma, 16)
                    nc.vector.tensor_scalar_mul(gamma_root[:, :], gamma_sb[:, :], ROOT_D).then_inc(s_gamma_root, 1)
                    floor_norm(FIRST)
                    dve.wait_ge(s_gamma_root, 1)
                    for c in range(C):
                        normalise_x(FIRST, 0, c, first=True)
                    for c in range(C):
                        split_xn(FIRST, 0, (c,))
                        qkva_lo_part(c)
                    floor_norm(FIRST + 1)
                    for c in range(C):
                        normalise_x(FIRST + 1, 1, c, first=True)
                    int_lo(0, gate_lo, gate_i, gate_hi)
                    split_xn(FIRST + 1, 1)
                if known == NB:
                    for k in range(2):
                        final_half(parity, k)
                elif has_final(known):
                    residual2(s, parity)
                if has_proj(known):
                    scan(s, 0)
                if known == FIRST + 1:
                    int_lo(1, up_lo, up_i, up_hi)
                if has_norm(known):
                    floor_norm(s)
                if has_final(known) and known not in (NB - 1, NB):
                    normalise2(s)
                if has_proj(known):
                    scan(s, 1)
                    times_q(s, 0)
                    times_q(s, 1)
                if known == FIRST + 1:
                    int_lo(2, down_lo, down_i, down_hi)
                if has_ffn(known):
                    hidden(s, 0)
                if known == NB - 1:
                    normalise2(s)
                if has_proj(known):
                    stats_r(s, known)
                if known == FIRST + 1:
                    dve.wait_ge(s_lo_sums, 3)
                    nc.vector.reduce_sum(lo_any[:, :], lo_sums[:, :], mybir.AxisListType.X).then_inc(s_lo_any0, 1)
                    dve.wait_ge(s_lo_any0, 1)
                    nc.vector.tensor_scalar_min(lo_any[:, :], lo_any[:, :], 1.0).then_inc(s_lo_any, 1)
                    dve.wait_ge(s_lo_count, 1)
                    nc.vector.tensor_scalar_min(lo_flag[:, :], ps[0:1, NPROJ - 1, 0:1], 1.0).then_inc(s_lo_flag, 1)
                if has_ffn(known):
                    hidden(s, 1)
                if has_proj(known):
                    normalise1(s, known, parity, (0, 1))
                if has_ffn(known):
                    hidden(s, 2)
                if has_proj(known):
                    normalise1(s, known, parity, (2, 3))
                if has_ffn(known):
                    hidden(s, 3)
                if has_norm(known):
                    for c in range(C):
                        normalise_x(s, parity, c)
                if has_ffn(known):
                    hidden(s, 4)
                if has_norm(known):
                    split_xn(s, parity)
                if has_ffn(known):
                    hidden(s, 5)
                if has_proj(known):
                    for c in range(C):
                        split_x1(s, c)

            run_steps(dve, step)

        @block.gpsimd
        def _(pool):
            pool.memset(ident[:, :], 0.0).then_inc(s_ident0, 1)
            pool.memset(minus_half[:, :], -0.5).then_inc(s_ident0, 1)
            pool.wait_ge(s_ident0, 2)
            pool.affine_select(out=ident[:, :], in_=ident[:, :], compare_op=ALU.not_equal, fill=1.0,
                               base=0, pattern=[[-1, P]], channel_multiplier=1).then_inc(s_ident, 1)
            pool.memset(ones[:, :], 1.0).then_inc(s_const, 1)

            def inverse_std(var, s_var, rstd, s_rstd, n, tiles=slice(0, TT)):
                pool.wait_ge(s_var, n)
                nc.gpsimd.tensor_tensor(out=rstd[:, tiles], in0=var[:, tiles], in1=minus_half[:, tiles], op=ALU.pow)\
                    .then_inc(s_rstd, 1)

            def inverse_norm(s):
                if not isinstance(s, int) or s >= 1:
                    pool.wait_ge(s_norms_out, 16 * s)
                if isinstance(s, int) and s in (-1, 0):
                    pool.wait_ge(s_first_norms, s + 2)
                pool.wait_ge(s_floor, s + 3)
                nc.gpsimd.tensor_tensor(out=inv_norm[:, :], in0=sum_sq_floor[:, :], in1=minus_half[:, :],
                                        op=ALU.pow).then_inc(s_inv_norm, 1)

            def residual1(s, parity, c):
                pool.wait_ge(s_qy, C * (s + 1) + c + 1)
                nc.gpsimd.tensor_tensor(out=r_fm[:, c, :], in0=qy[:, c, :], in1=xf_in[:, (parity + 1) % 2, c, :],
                                        op=ALU.add).then_inc(s_r_fm, 1)

            def split_h(s, p):
                pool.wait_ge(s_h_hi, HC * s + p + 1)
                nc.gpsimd.tensor_tensor(out=h_lo[:, p, :], in0=h[:, p % 2, :], in1=wide(h_hi[:, p, :]),
                                        op=ALU.subtract).then_inc(s_h_lo, 1)

            def step(s, known, parity):
                if known == FIRST:
                    inverse_norm(FIRST)
                    inverse_norm(FIRST + 1)
                if known == NB:
                    for k in range(2):
                        inverse_std(var2, s_var2, rstd2, s_rstd2, NB + k, slice(2 * k, 2 * k + 2))
                elif has_final(known):
                    inverse_std(var2, s_var2, rstd2, s_rstd2, s)
                if has_norm(known):
                    inverse_norm(s)
                if has_proj(known):
                    residual1(s, parity, 0)
                    residual1(s, parity, 1)
                if has_ffn(known):
                    split_h(s, 0)
                if has_proj(known):
                    inverse_std(var1, s_var1, rstd1, s_rstd1, s + 2)
                if has_ffn(known):
                    for p in range(1, HC):
                        split_h(s, p)

            run_steps(pool, step)


def kernel(L0_attn_x, L0_attn_W_qkva, L0_attn_gamma, L0_ffn_w_gate, L0_ffn_w_up, L0_ffn_w_down):
    import numpy as np
    import concourse.bacc as bacc
    from concourse.bass_utils import run_bass_kernel_spmd

    P = 128
    x = np.asarray(L0_attn_x)
    nb, n, d = x.shape

    def by_partition(w):
        w = np.asarray(w)
        return np.ascontiguousarray(w.T.reshape(-1, P, w.shape[0]).transpose(1, 0, 2))

    arrays = {
        "x_rows": np.ascontiguousarray(x.reshape(nb, P, n // P, d)),
        "x_fm": np.ascontiguousarray(x.transpose(0, 2, 1).reshape(nb, d // P, P, n).transpose(0, 2, 1, 3)),
        "w_qkva": by_partition(L0_attn_W_qkva),
        "gamma": np.ascontiguousarray(np.asarray(L0_attn_gamma).reshape(d // P, P).T),
        "w_gate": by_partition(L0_ffn_w_gate),
        "w_up": by_partition(L0_ffn_w_up),
        "w_down": by_partition(L0_ffn_w_down),
    }
    nc = bacc.Bacc("TRN2", target_bir_lowering=False, num_devices=1)
    args = [nc.dram_tensor(name, a.shape, mybir.dt.from_np(a.dtype), kind="ExternalInput").ap()
            for name, a in arrays.items()]
    out = nc.dram_tensor("out", arrays["x_rows"].shape, mybir.dt.float32, kind="ExternalOutput").ap()
    norms = nc.dram_tensor("norms", (2, P, n // P), mybir.dt.float32, kind="Internal").ap()
    post_norm_scan_ffn(nc, *args, norms, out)
    r = run_bass_kernel_spmd(nc, [arrays], core_ids=[0])
    got = np.asarray(r.results[0]["out"])
    return np.ascontiguousarray(got.transpose(0, 2, 1, 3).reshape(nb, n, d))
```

```python
import concourse.bass as bass
from concourse import mybir
from contextlib import ExitStack


def post_norm_scan_ffn(nc, x_rows, x_fm, w_qkva, gamma, w_gate, w_up, w_down, norms_dram, stats_dram, out):
    fp32, fp32r, i32 = mybir.dt.float32, mybir.dt.float32r, mybir.dt.int32
    ALU, ACT = mybir.AluOpType, mybir.ActivationFunctionType

    P = 128
    NB, _, TT, D = x_rows.shape
    N = TT * P
    C = D // P
    E = w_qkva.shape[2]
    H = w_gate.shape[2]
    HC = H // P
    DEQUANT = 1.0 / 127.0
    LN_EPS = 1e-5
    NORM_EPS = 1e-12
    ROOT_D = float(D) ** 0.5

    Q, KV, A = 0, 1, 2
    PROJ = [(A, 0), (KV, 0), (A, 1), (KV, 1), (Q, 0), (Q, 1)]
    NPROJ = len(PROJ)
    A_AT, KV_AT, Q_AT = [0, 2], [1, 3], [4, 5]
    R_BANK = 2
    NORM_BANK = 6
    DOWN_BANK = 4
    STAT_BANK = 4
    X1_BANK = 6
    GU_BANK = [6, 0]

    FIRST, LAST = -2, NB
    LOOP = range(1, NB - 3, 2)

    def has_proj(s):
        return s is None or 0 <= s + 1 < NB

    def has_ffn(s):
        return s is None or 0 <= s < NB

    def has_norm(s):
        return s is None or 0 <= s < NB - 2

    def has_final(s):
        return s is None or 0 <= s - 1 < NB

    def has_load(s):
        return s is None or 2 <= s + 3 < NB

    def has_late_x1(s):
        return s is None or 1 <= s < NB

    def run_steps(eng, step, first=0):
        for s in range(first, LOOP.start):
            step(s, s, s % 2)
        with eng.Fori(LOOP.start, LOOP[-1] + 1, LOOP.step) as s:
            for k in range(LOOP.step):
                step(s + k, None, (LOOP.start + k) % 2)
        for s in range(LOOP[-1] + LOOP.step, LAST + 1):
            step(s, s, s % 2)

    ctx = ExitStack()
    with ctx:
        def sb(name, shape, dt=fp32):
            return ctx.enter_context(nc.sbuf_tensor(name, shape, dt))

        def sem(name):
            return ctx.enter_context(nc.semaphore(name))

        qkva_raw = sb("qkva_raw", [P, C, E])
        gamma_sb = sb("gamma_sb", [P, C])
        gamma_root = sb("gamma_root", [P, C])
        qkva_hi, qkva_lo = sb("qkva_hi", [P, C, E], fp32r), sb("qkva_lo", [P, C, E], fp32r)
        gate_i, up_i = sb("gate_i", [P, C, H], i32), sb("up_i", [P, C, H], i32)
        down_i = sb("down_i", [P, HC, D], i32)
        gate_hi, gate_lo = sb("gate_hi", [P, C, H], fp32r), sb("gate_lo", [P, C, H], fp32r)
        up_hi, up_lo = sb("up_hi", [P, C, H], fp32r), sb("up_lo", [P, C, H], fp32r)
        down_hi, down_lo = sb("down_hi", [P, HC, D], fp32r), sb("down_lo", [P, HC, D], fp32r)
        lo_sums = sb("lo_sums", [P, 3])
        lo_any = sb("lo_any", [P, 1])
        lo_flag = sb("lo_flag", [1, 1], i32)
        ident = sb("ident", [P, P])
        ones = sb("ones", [P, 1])
        table_probe = sb("table_probe", [P, 1])
        minus_half = sb("minus_half", [P, TT])
        xn_in = sb("xn_in", [P, 2, TT, D])
        xf_in = sb("xf_in", [P, 2, C, N])
        sum_sq = sb("sum_sq", [P, TT])
        sum_sq_floor = sb("sum_sq_floor", [P, TT])
        inv_norm = sb("inv_norm", [P, TT])
        xn = sb("xn", [P, C, N])
        norm_rows = sb("norm_rows", [P, N])
        xn_hi, xn_lo = sb("xn_hi", [P, 2, C, N], fp32r), sb("xn_lo", [P, 2, C, N], fp32r)
        decay = sb("decay", [P, C, N])
        y = sb("y", [P, C, N])
        r_fm = sb("r_fm", [P, C, N])
        stats1, mv1 = sb("stats1", [P, TT, 6]), sb("mv1", [P, 2, TT])
        var1 = sb("var1", [P, TT])
        stat_tiles = sb("stat_tiles", [2 * TT, P])
        stat_rows = sb("stat_rows", [P, 2, N])
        x1_fm = sb("x1_fm", [P, C, N])
        x1 = sb("x1", [P, 2, TT, D])
        x1_hi, x1_lo = sb("x1_hi", [P, C, N], fp32r), sb("x1_lo", [P, C, N], fp32r)
        silu_g = sb("silu_g", [P, 2, N])
        h = sb("h", [P, 2, N])
        h_hi, h_lo = sb("h_hi", [P, HC, N], fp32r), sb("h_lo", [P, HC, N], fp32r)
        r2 = sb("r2", [P, TT, D])
        stats2, mv2 = sb("stats2", [P, TT, 6]), sb("mv2", [P, 2, TT])
        var2, rstd2 = sb("var2", [P, TT]), sb("rstd2", [P, TT])
        out_sb = sb("out_sb", [P, TT, D])

        ps = ctx.enter_context(nc.psum_tensor("ps", [P, 8, N], fp32))

        s_xn_in = [sem("s_xn_in0"), sem("s_xn_in1")]
        s_xf_in = [sem("s_xf_in0"), sem("s_xf_in1")]
        s_w_qkva, s_gamma = sem("s_w_qkva"), sem("s_gamma")
        s_w_gate, s_w_up, s_w_down = sem("s_w_gate"), sem("s_w_up"), sem("s_w_down")
        s_norms_out, s_norm_rows = sem("s_norms_out"), sem("s_norm_rows")
        s_stored = sem("s_stored")
        s_ident0, s_ident, s_const = sem("s_ident0"), sem("s_ident"), sem("s_const")
        s_gamma_root, s_qkva_hi, s_qkva_lo = sem("s_gamma_root"), sem("s_qkva_hi"), sem("s_qkva_lo")
        s_int_hi, s_up_f = sem("s_int_hi"), sem("s_up_f")
        s_gate_lo, s_up_lo, s_down_lo = sem("s_gate_lo"), sem("s_up_lo"), sem("s_down_lo")
        s_lo_sums, s_lo_any0, s_lo_any = sem("s_lo_sums"), sem("s_lo_any0"), sem("s_lo_any")
        s_lo_count, s_lo_flag = sem("s_lo_count"), sem("s_lo_flag")
        s_sum_sq, s_floor, s_inv_norm = sem("s_sum_sq"), sem("s_floor"), sem("s_inv_norm")
        s_first_norms, s_xn, s_xn_hi, s_xn_lo = sem("s_first_norms"), sem("s_xn"), sem("s_xn_hi"), sem("s_xn_lo")
        s_proj = sem("s_proj")
        s_tanh, s_decay, s_y, s_qy, s_r_fm = (sem(f"s_{n}") for n in ("tanh", "decay", "y", "qy", "r_fm"))
        s_r = sem("s_r")
        s_stats1, s_mv1, s_var1, s_rstd1 = (sem(f"s_{n}") for n in ("stats1", "mv1", "var1", "rstd1"))
        s_x1 = sem("s_x1")
        s_stat_t, s_stat_tiles = sem("s_stat_t"), sem("s_stat_tiles")
        s_stats_out, s_stat_rows = sem("s_stats_out"), sem("s_stat_rows")
        s_centred, s_x1_fm = sem("s_centred"), sem("s_x1_fm")
        s_x1_fm0 = sem("s_x1_fm0")
        s_x1_hi, s_x1_lo = sem("s_x1_hi"), sem("s_x1_lo")
        s_gu = sem("s_gu")
        s_silu, s_h, s_h_hi, s_h_lo = sem("s_silu"), sem("s_h"), sem("s_h_hi"), sem("s_h_lo")
        s_last_h_lo = sem("s_last_h_lo")
        s_down, s_r2 = sem("s_down"), sem("s_r2")
        s_stats2, s_mv2, s_var2, s_rstd2 = (sem(f"s_{n}") for n in ("stats2", "mv2", "var2", "rstd2"))
        s_out = sem("s_out")

        def wide(ap):
            return ap.bitcast(fp32)

        block = ctx.enter_context(nc.Block())

        @block.sync
        def _(sp):
            norms_flat = norms_dram.rearrange("b p t -> b (p t)")

            def norms_to_rows(b, parity):
                sp.wait_ge(s_inv_norm, b + 1)
                sp.dma_start(norms_dram[parity], inv_norm[:, :]).then_inc(s_norms_out, 16)
                sp.wait_ge(s_norms_out, 16 * (b - 1))
                sp.dma_start(norm_rows[:, :], norms_flat[parity:parity + 1, :].to_broadcast([P, N]))\
                    .then_inc(s_norm_rows, 16)

            def stats_to_rows(b, parity):
                sp.wait_ge(s_stat_tiles, b)
                sp.dma_start(stats_dram[parity], stat_tiles[:, :]).then_inc(s_stats_out, 16)
                sp.wait_ge(s_stats_out, 16 * b)
                sp.dma_start(stat_rows[:, :, :], stats_flat[parity:parity + 1, :].to_broadcast([P, 2 * N]))\
                    .then_inc(s_stat_rows, 16)

            stats_flat = stats_dram.rearrange("b r n -> b (r n)")
            sp.dma_start(xn_in[:, 0, :, :], x_rows[0]).then_inc(s_xn_in[0], 16)
            sp.dma_start(qkva_raw[:, :, :], w_qkva).then_inc(s_w_qkva, 16)
            sp.dma_start(xf_in[:, 0, :, :], x_fm[0]).then_inc(s_xf_in[0], 16)
            sp.dma_start(xn_in[:, 1, :, :], x_rows[1]).then_inc(s_xn_in[1], 16)
            sp.dma_start(gate_i[:, :, :], w_gate).then_inc(s_w_gate, 16)
            sp.dma_start(xf_in[:, 1, :, :], x_fm[1]).then_inc(s_xf_in[1], 16)
            sp.dma_start(up_i[:, :, :], w_up).then_inc(s_w_up, 16)
            sp.dma_start(down_i[:, :, :], w_down).then_inc(s_w_down, 16)

            def step(s, known, parity):
                if has_load(known):
                    sp.wait_ge(s_sum_sq, s + 2)
                    sp.dma_start(xn_in[:, (parity + 1) % 2, :, :], x_rows[s + 3])\
                        .then_inc(s_xn_in[(parity + 1) % 2], 16)
                if has_norm(known):
                    norms_to_rows(s + 2, parity)
                if has_load(known):
                    sp.wait_ge(s_r_fm, C * (s + 2))
                    sp.dma_start(xf_in[:, (parity + 1) % 2, :, :], x_fm[s + 3])\
                        .then_inc(s_xf_in[(parity + 1) % 2], 16)
                if has_proj(known) and known != -1:
                    stats_to_rows(s + 1, (parity + 1) % 2)
                if known == NB:
                    for k in range(2):
                        sp.wait_ge(s_out, NB + k)
                        sp.dma_start(out[NB - 1][:, 2 * k:2 * k + 2, :], out_sb[:, 2 * k:2 * k + 2, :])\
                            .then_inc(s_stored, 16)
                elif has_final(known):
                    sp.wait_ge(s_out, s)
                    sp.dma_start(out[s - 1], out_sb[:, :, :]).then_inc(s_stored, 16)

            run_steps(sp, step, FIRST)
            sp.wait_ge(s_stored, 16 * (NB + 1))

        @block.tensor
        def _(pe):
            def proj(s, known, outputs=range(NPROJ)):
                x_parity = (s + 1) % 2 if known is not None else (parity_now + 1) % 2
                batch0_read = [(s_tanh, 1), (s_y, 1), (s_tanh, 2), (s_y, 2), (s_qy, 1), (s_qy, 2)]
                for n in outputs:
                    part, c = PROJ[n]
                    if known == 0:
                        pe.wait_ge(*batch0_read[n])
                    if n == DOWN_BANK and has_final(known):
                        pe.wait_ge(s_r2, 2 * s - 1)
                    if n == DOWN_BANK + 1 and has_final(known):
                        pe.wait_ge(s_r2, 2 * s)
                    e = part * D + c * P
                    for k in range(C):
                        for w, x_ in ((qkva_hi, xn_hi), (qkva_hi, xn_lo), (qkva_lo, xn_hi)):
                            if n == 0 and w is qkva_hi:
                                pe.wait_ge(s_xn_hi if x_ is xn_hi else s_xn_lo, C * (s + 1) + k + 1)
                            if n == 0 and known == -1 and x_ is xn_hi:
                                pe.wait_ge(s_qkva_hi if w is qkva_hi else s_qkva_lo, k + 1)
                            last = nc.tensor.matmul(ps[:, n, :], w[:, k, e:e + P], x_[:, x_parity, k, :],
                                                    start=(k == 0 and w is qkva_hi and x_ is xn_hi),
                                                    stop=(k == C - 1 and w is qkva_lo))
                    last.then_inc(s_proj, 1)

            def r_to_nat(s, bank, chunks=range(C)):
                for c in chunks:
                    pe.wait_ge(s_r_fm, C * (s + 1) + c + 1)
                    for t in range(TT):
                        o = (t % 2) * D + c * P
                        last = nc.tensor.transpose(ps[:, bank + t // 2, o:o + P],
                                                   r_fm[:, c, t * P:(t + 1) * P], ident[:, :])
                        if c == C - 1 and t % 2:
                            last.then_inc(s_r, 1)

            def spread_norms(b):
                pe.wait_ge(s_inv_norm, b + 1)
                pe.wait_ge(s_ident, 1)
                for t in range(TT):
                    last = nc.tensor.transpose(ps[:, NORM_BANK + b, t:N:TT],
                                               inv_norm[:, t:t + 1].to_broadcast([P, P]), ident[:, :])
                last.then_inc(s_first_norms, 1)

            def x1_to_fm():
                pe.wait_ge(s_x1, TT)
                for c in range(C):
                    for t in range(TT):
                        last = nc.tensor.transpose(ps[:, X1_BANK + c, t * P:(t + 1) * P],
                                                   x1[:, 0, t, c * P:(c + 1) * P], ident[:, :])
                    last.then_inc(s_x1_fm0, 1)

            def transpose_stats(s):
                pe.wait_ge(s_rstd1, s + 2)
                nc.tensor.transpose(ps[0:2 * TT, STAT_BANK, 0:P], mv1[:, :, :].rearrange("p a t -> p (a t)"),
                                    ident[:, :]).then_inc(s_stat_t, 1)

            def gate_up(s, known, p, general, which=(0, 1)):
                if p == 0 and known == 0:
                    pe.wait_ge(s_x1_lo, C)
                if p == 1 and has_proj(known) and 0 in which:
                    pe.wait_ge(s_y, C * (s + 1) + 1)
                if p >= 2 and 0 in which:
                    pe.wait_ge(s_h, HC * s + p - 1)
                for n in which:
                    hi, lo = ((gate_hi, gate_lo), (up_hi, up_lo))[n]
                    passes = [(w, x_, k) for w in ((hi, lo) if general else (hi,))
                              for k in range(C) for x_ in (x1_hi, x1_lo)]
                    for m, (w, x_, k) in enumerate(passes):
                        if p == 0 and n == 0 and w is hi:
                            pe.wait_ge(s_x1_hi if x_ is x1_hi else s_x1_lo, C * s + k + 1)
                        last = nc.tensor.matmul(ps[:, GU_BANK[p % 2] + n, :], w[:, k, p * P:(p + 1) * P],
                                                x_[:, k, :], start=(m == 0), stop=(m == len(passes) - 1))
                    last.then_inc(s_gu, 1)

            def down(s, known, general):
                if has_proj(known):
                    pe.wait_ge(s_stat_tiles, s + 1)
                halves = ((0, 1), (2, 3)) if known == NB - 1 else ((0, 1, 2, 3),)
                for tiles in halves:
                    for k in range(HC):
                        passes = [(h_, w) for w in ((down_hi, down_lo) if general else (down_hi,))
                                  for h_ in (h_hi, h_lo)]
                        for m, (h_, w) in enumerate(passes):
                            if 0 in tiles and w is down_hi:
                                if h_ is h_lo and known == NB - 1 and k == HC - 1:
                                    pe.wait_ge(s_last_h_lo, 1)
                                else:
                                    pe.wait_ge(s_h_hi if h_ is h_hi else s_h_lo, HC * s + k + 1)
                            for t in tiles:
                                o = (t % 2) * D
                                last = nc.tensor.matmul(
                                    ps[:, DOWN_BANK + t // 2, o:o + D], h_[:, k, t * P:(t + 1) * P], w[:, k, :],
                                    start=(k == 0 and t % 2 == 0 and m == 0),
                                    stop=(k == HC - 1 and m == len(passes) - 1), skip_group_check=True)
                                if k == HC - 1 and m == len(passes) - 1 and t % 2:
                                    last.then_inc(s_down, 1)

            def steps(general):
                def step(s, known, parity):
                    nonlocal parity_now
                    parity_now = parity
                    if has_proj(known) and known != 0:
                        proj(s, known)
                    if not has_ffn(known):
                        return
                    gate_up(s, known, 0, general)
                    if has_proj(known):
                        r_to_nat(s, R_BANK, (0,))
                    gate_up(s, known, 1, general, (0,))
                    if has_proj(known):
                        r_to_nat(s, R_BANK, (1,))
                    gate_up(s, known, 1, general, (1,))
                    gate_up(s, known, 2, general)
                    gate_up(s, known, 3, general)
                    if has_proj(known):
                        transpose_stats(s)
                    gate_up(s, known, 4, general)
                    gate_up(s, known, 5, general)
                    down(s, known, general)
                return step

            parity_now = 0
            spread_norms(0)
            proj(-1, -1, range(0, 2))
            spread_norms(1)
            proj(-1, -1, range(2, NPROJ))
            proj(0, 0, range(0, 1))
            pe.wait_ge(s_xn, C * 2)
            r_to_nat(-1, X1_BANK)
            proj(0, 0, range(1, NPROJ - 1))
            pe.wait_ge(s_lo_any, 1)
            pe.wait_ge(s_const, 1)
            pe.wait_ge(s_qy, C)
            nc.tensor.matmul(ps[0:1, NPROJ - 1, 0:1], lo_any[:, :], ones[:, :],
                             start=True, stop=True).then_inc(s_lo_count, 1)
            x1_to_fm()
            pe.wait_ge(s_lo_flag, 1)
            proj(0, 0, range(NPROJ - 1, NPROJ))
            flag = pe.value_load(lo_flag[0:1, 0:1], min_val=0, max_val=1)
            with pe.If(flag == 0):
                run_steps(pe, steps(False))
            with pe.Else():
                run_steps(pe, steps(True))

        @block.scalar
        def _(act):
            act.dma_start(gamma_sb[:, :], gamma).then_inc(s_gamma, 16)
            act.wait_ge(s_const, 1)
            nc.scalar.activation(table_probe[:, :], ones[:, :], ACT.Silu)

            def tanh(s, c):
                act.wait_ge(s_proj, NPROJ * (s + 1) + A_AT[c] + 1)
                nc.scalar.activation(decay[:, c, :], ps[:, A_AT[c], :], ACT.Tanh, scale=0.5).then_inc(s_tanh, 1)

            def sum_squares(s, parity):
                act.wait_ge(s_xn_in[parity], 8 * (s + 4 - parity))
                if not isinstance(s, int) or s >= -1:
                    act.wait_ge(s_floor, s + 2)
                for t in range(TT):
                    last = nc.scalar.activation(xn_in[:, parity, t, :], xn_in[:, parity, t, :], ACT.Square,
                                                accum_out=sum_sq[:, t:t + 1])
                last.then_inc(s_sum_sq, 1)

            def split_xn(s, parity):
                for c in range(C):
                    act.wait_ge(s_xn, C * (s + 2) + c + 1)
                    nc.scalar.activation(xn_hi[:, parity, c, :], xn[:, c, :], ACT.Copy).then_inc(s_xn_hi, 1)

            def int_hi(n, hi, raw, loaded):
                act.wait_ge(loaded, 16)
                nc.scalar.activation(hi[:, :, :], raw[:, :, :], ACT.Copy).then_inc(s_int_hi, 1)

            def up_to_float():
                nc.scalar.activation(wide(up_i[:, :, :]), up_i[:, :, :], ACT.Copy).then_inc(s_up_f, 1)

            def int_lo_sum(n, lo, raw, s_lo, parts=1):
                act.wait_ge(s_lo, parts)
                nc.scalar.activation(wide(raw[:, :, :]), wide(lo[:, :, :]), ACT.Square,
                                     accum_out=lo_sums[:, n:n + 1]).then_inc(s_lo_sums, 1)

            def silu(s, p):
                act.wait_ge(s_gu, 2 * HC * s + 2 * p + 1)
                nc.scalar.activation(silu_g[:, p % 2, :], ps[:, GU_BANK[p % 2], :], ACT.Silu,
                                     scale=DEQUANT).then_inc(s_silu, 1)

            def split_h(s, p):
                act.wait_ge(s_h, HC * s + p + 1)
                nc.scalar.activation(h_hi[:, p, :], h[:, p % 2, :], ACT.Copy).then_inc(s_h_hi, 1)

            def split_x1(s, known, c):
                if known == -1:
                    act.wait_ge(s_x1_fm0, c + 1)
                else:
                    act.wait_ge(s_x1_fm, C * s + c + 1)
                src = ps[:, X1_BANK + c, :] if known == -1 else x1_fm[:, c, :]
                nc.scalar.activation(x1_hi[:, c, :], src, ACT.Copy).then_inc(s_x1_hi, 1)

            def copy_stats(s):
                act.wait_ge(s_stat_t, s + 1)
                nc.scalar.activation(stat_tiles[:, :], ps[0:2 * TT, STAT_BANK, 0:P], ACT.Copy).then_inc(s_stat_tiles, 1)

            def step(s, known, parity):
                if has_proj(known) and known != 0:
                    tanh(s, 0)
                    tanh(s, 1)
                if has_norm(known):
                    sum_squares(s, parity)
                if has_ffn(known):
                    silu(s, 0)
                    split_h(s, 0)
                    silu(s, 1)
                    for p in range(2, HC - 1):
                        silu(s, p)
                        split_h(s, p - 1)
                        if p == 3 and has_proj(known):
                            copy_stats(s)
                if has_norm(known):
                    split_xn(s, parity)
                if has_ffn(known):
                    silu(s, HC - 1)
                    split_h(s, HC - 2)
                    split_h(s, HC - 1)
                if has_proj(known):
                    for c in range(C):
                        split_x1(s, known, c)

            sum_squares(-2, 0)
            act.wait_ge(s_w_qkva, 16)
            act.wait_ge(s_gamma_root, 1)
            for c in range(C):
                nc.scalar.activation(qkva_hi[:, c, :], qkva_raw[:, c, :], ACT.Copy,
                                     scale=gamma_root[:, c:c + 1]).then_inc(s_qkva_hi, 1)
            split_xn(-2, 0)
            sum_squares(-1, 1)
            int_hi(0, gate_hi, gate_i, s_w_gate)
            tanh(-1, 0)
            int_hi(1, up_hi, up_i, s_w_up)
            split_xn(-1, 1)
            tanh(-1, 1)
            up_to_float()
            int_hi(2, down_hi, down_i, s_w_down)
            int_lo_sum(0, gate_lo, gate_i, s_gate_lo)
            int_lo_sum(1, up_lo, up_i, s_up_lo)
            int_lo_sum(2, down_lo, down_i, s_down_lo, 2)
            for c in range(C):
                tanh(0, c)
            for c in range(C):
                split_x1(-1, -1, c)
            run_steps(act, step)

        @block.vector
        def _(dve):
            def row_stats(n, rows, s_rows, stats, s_stats, mv, s_mv, var, s_var, between=None):
                for t in range(TT):
                    if t % 2 == 0:
                        dve.wait_ge(s_rows, 2 * (n - 1) + t // 2 + 1)
                    if t == 2:
                        dve.wait_ge(s_stats, TT * (n - 1) + 2)
                    nc.vector.bn_stats(stats[:, t, :], rows(t)).then_inc(s_stats, 1)
                    if t == 2:
                        nc.vector.bn_aggr(mv[:, :, 0], stats[:, 0, :])
                        nc.vector.bn_aggr(mv[:, :, 1], stats[:, 1, :]).then_inc(s_mv, 1)
                if between is not None:
                    between()
                dve.wait_ge(s_stats, TT * n)
                dve.wait_ge(s_mv, 2 * n - 1)
                nc.vector.tensor_scalar_add(var[:, 0:2], mv[:, 1, 0:2], LN_EPS)
                nc.vector.bn_aggr(mv[:, :, 2], stats[:, 2, :])
                nc.vector.bn_aggr(mv[:, :, 3], stats[:, 3, :]).then_inc(s_mv, 1)
                dve.wait_ge(s_mv, 2 * n)
                nc.vector.tensor_scalar_add(var[:, 2:4], mv[:, 1, 2:4], LN_EPS).then_inc(s_var, 1)

            def residual2(s, parity):
                for k in range(2):
                    dve.wait_ge(s_down, 2 * s - 1 + k)
                    nc.vector.scalar_tensor_tensor(
                        out=r2[:, 2 * k:2 * k + 2, :].rearrange("p t d -> p (t d)"), in0=ps[:, DOWN_BANK + k, :],
                        scalar=DEQUANT, op0=ALU.mult,
                        in1=x1[:, (parity + 1) % 2, 2 * k:2 * k + 2, :].rearrange("p t d -> p (t d)"),
                        op1=ALU.add).then_inc(s_r2, 1)

            def stats2_rows(s, between=None):
                row_stats(s, lambda t: r2[:, t, :], s_r2, stats2, s_stats2, mv2, s_mv2, var2, s_var2, between)

            def final_half(parity, k):
                tiles = (2 * k, 2 * k + 1)
                dve.wait_ge(s_down, 2 * (NB - 1) + k + 1)
                nc.vector.scalar_tensor_tensor(
                    out=r2[:, 2 * k:2 * k + 2, :].rearrange("p t d -> p (t d)"), in0=ps[:, DOWN_BANK + k, :],
                    scalar=DEQUANT, op0=ALU.mult,
                    in1=x1[:, (parity + 1) % 2, 2 * k:2 * k + 2, :].rearrange("p t d -> p (t d)"),
                    op1=ALU.add).then_inc(s_r2, 1)
                dve.wait_ge(s_r2, 2 * (NB - 1) + k + 1)
                for t in tiles:
                    last = nc.vector.bn_stats(stats2[:, t, :], r2[:, t, :])
                last.then_inc(s_stats2, 1)
                dve.wait_ge(s_stats2, TT * (NB - 1) + k + 1)
                for t in tiles:
                    last = nc.vector.bn_aggr(mv2[:, :, t], stats2[:, t, :])
                last.then_inc(s_mv2, 1)
                dve.wait_ge(s_mv2, 2 * (NB - 1) + k + 1)
                nc.vector.tensor_scalar_add(var2[:, 2 * k:2 * k + 2], mv2[:, 1, 2 * k:2 * k + 2], LN_EPS)\
                    .then_inc(s_var2, 1)
                dve.wait_ge(s_rstd2, NB - 1 + k + 1)
                if k == 0:
                    dve.wait_ge(s_stored, 16 * (NB - 1))
                for t in tiles:
                    last = nc.vector.tensor_scalar(out_sb[:, t, :], r2[:, t, :], mv2[:, 0, t:t + 1], rstd2[:, t:t + 1],
                                                   ALU.subtract, ALU.mult)
                last.then_inc(s_out, 1)

            def normalise2(s):
                dve.wait_ge(s_rstd2, s)
                if not isinstance(s, int) or s >= 2:
                    dve.wait_ge(s_stored, 16 * (s - 1))
                for t in range(TT):
                    last = nc.vector.tensor_scalar(out_sb[:, t, :], r2[:, t, :], mv2[:, 0, t:t + 1], rstd2[:, t:t + 1],
                                                   ALU.subtract, ALU.mult)
                last.then_inc(s_out, 1)

            def scan(s, c):
                n = C * (s + 1) + c + 1
                dve.wait_ge(s_tanh, n)
                nc.vector.tensor_scalar(decay[:, c, :], decay[:, c, :], 0.5, 0.5, ALU.mult, ALU.add)\
                    .then_inc(s_decay, 1)
                dve.wait_ge(s_proj, NPROJ * (s + 1) + KV_AT[c] + 1)
                dve.wait_ge(s_decay, n)
                nc.vector.tensor_tensor_scan(out=y[:, c, :], data0=decay[:, c, :], data1=ps[:, KV_AT[c], :],
                                             initial=0.0, op0=ALU.mult, op1=ALU.add).then_inc(s_y, 1)

            def times_q(s, c):
                dve.wait_ge(s_proj, NPROJ * (s + 1) + Q_AT[c] + 1)
                dve.wait_ge(s_y, C * (s + 1) + c + 1)
                nc.vector.tensor_tensor(out=y[:, c, :], in0=ps[:, Q_AT[c], :], in1=y[:, c, :], op=ALU.mult)\
                    .then_inc(s_qy, 1)

            def r_rows(known, t):
                bank = (X1_BANK if known == -1 else R_BANK) + t // 2
                return ps[:, bank, (t % 2) * D:(t % 2 + 1) * D]

            def stats_r(s, known):
                row_stats(s + 2, lambda t: r_rows(known, t), s_r,
                          stats1, s_stats1, mv1, s_mv1, var1, s_var1,
                          between=(lambda: hidden(s, 1)) if has_ffn(known) else None)

            def normalise1(s, known, parity, tiles):
                dve.wait_ge(s_rstd1, s + 2)
                for t in tiles:
                    nc.vector.tensor_scalar(x1[:, (parity + 1) % 2, t, :], r_rows(known, t),
                                            mv1[:, 0, t:t + 1], mv1[:, 1, t:t + 1],
                                            ALU.subtract, ALU.mult).then_inc(s_x1, 1)

            def hidden(s, p):
                dve.wait_ge(s_gu, 2 * HC * s + 2 * p + 2)
                dve.wait_ge(s_silu, HC * s + p + 1)
                if p >= 2:
                    dve.wait_ge(s_h_hi, HC * s + p - 1)
                    dve.wait_ge(s_h_lo, HC * s + p - 1)
                nc.vector.scalar_tensor_tensor(out=h[:, p % 2, :], in0=ps[:, GU_BANK[p % 2] + 1, :], scalar=DEQUANT,
                                               op0=ALU.mult, in1=silu_g[:, p % 2, :], op1=ALU.mult)\
                    .then_inc(s_h, 1)

            def split_h(s, p):
                dve.wait_ge(s_h_hi, HC * s + p + 1)
                nc.vector.tensor_tensor(out=h_lo[:, p, :], in0=h[:, p % 2, :], in1=wide(h_hi[:, p, :]),
                                        op=ALU.subtract).then_inc(s_last_h_lo, 1)

            def floor_norm(s):
                dve.wait_ge(s_sum_sq, s + 3)
                nc.vector.tensor_scalar_max(sum_sq_floor[:, :], sum_sq[:, :], NORM_EPS ** 2).then_inc(s_floor, 1)

            def normalise_x(s, parity, c, first=False):
                if c == 0:
                    dve.wait_ge(s_xf_in[parity], 8 * (s + 4 - parity))
                    if first:
                        dve.wait_ge(s_first_norms, s + 3)
                    else:
                        dve.wait_ge(s_norm_rows, 16 * (s + 1))
                norms = ps[:, NORM_BANK + parity, :] if first else norm_rows[:, :]
                nc.vector.tensor_tensor(out=xn[:, c, :], in0=xf_in[:, parity, c, :], in1=norms,
                                        op=ALU.mult).then_inc(s_xn, 1)

            def split_xn(s, parity, chunks=range(C)):
                for c in chunks:
                    dve.wait_ge(s_xn_hi, C * (s + 2) + c + 1)
                    nc.vector.tensor_tensor(out=xn_lo[:, parity, c, :], in0=xn[:, c, :],
                                            in1=wide(xn_hi[:, parity, c, :]), op=ALU.subtract)\
                        .then_inc(s_xn_lo, 1)

            def qkva_lo_part(c):
                dve.wait_ge(s_qkva_hi, c + 1)
                nc.vector.scalar_tensor_tensor(out=qkva_lo[:, c, :], in0=qkva_raw[:, c, :],
                                               scalar=gamma_root[:, c:c + 1], op0=ALU.mult,
                                               in1=wide(qkva_hi[:, c, :]), op1=ALU.subtract)\
                    .then_inc(s_qkva_lo, 1)

            def int_lo(n, lo, raw, hi, s_lo, chunks):
                dve.wait_ge(s_int_hi, n + 1)
                nc.vector.tensor_tensor(out=lo[:, chunks, :], in0=raw[:, chunks, :], in1=wide(hi[:, chunks, :]),
                                        op=ALU.subtract).then_inc(s_lo, 1)

            def normalise_fm(s):
                dve.wait_ge(s_stat_rows, 16 * (s + 1))
                for c in range(C):
                    nc.vector.tensor_tensor(out=r_fm[:, c, :], in0=r_fm[:, c, :], in1=stat_rows[:, 0, :],
                                            op=ALU.subtract).then_inc(s_centred, 1)
                for c in range(C):
                    scale_x1(s, c)

            def add_x(s, parity, c):
                dve.wait_ge(s_qy, C * (s + 1) + c + 1)
                nc.vector.tensor_tensor(out=r_fm[:, c, :], in0=y[:, c, :], in1=xf_in[:, (parity + 1) % 2, c, :],
                                        op=ALU.add).then_inc(s_r_fm, 1)

            def scale_x1(s, c):
                dve.wait_ge(s_centred, C * s + c + 1)
                nc.vector.tensor_tensor(out=x1_fm[:, c, :], in0=r_fm[:, c, :], in1=stat_rows[:, 1, :],
                                        op=ALU.mult).then_inc(s_x1_fm, 1)

            def split_x1(b, known, c):
                dve.wait_ge(s_x1_hi, C * b + c + 1)
                src = ps[:, X1_BANK + c, :] if known == -1 else x1_fm[:, c, :]
                nc.vector.tensor_tensor(out=x1_lo[:, c, :], in0=src, in1=wide(x1_hi[:, c, :]),
                                        op=ALU.subtract).then_inc(s_x1_lo, 1)

            def step(s, known, parity):
                if known == NB:
                    for k in range(2):
                        final_half(parity, k)
                elif has_final(known):
                    if known == NB - 1:
                        for c in range(C):
                            split_x1(s, known, c)
                    residual2(s, parity)
                    if known == NB - 1:
                        hidden(s, 0)
                        stats2_rows(s, between=lambda: hidden(s, 1))
                    else:
                        stats2_rows(s)
                if has_proj(known):
                    if known != 0:
                        scan(s, 0)
                    scan(s, 1)
                if has_late_x1(known) and known != NB - 1:
                    for c in range(C):
                        split_x1(s, known, c)
                if has_norm(known):
                    floor_norm(s)
                if has_proj(known):
                    for c in range(C):
                        times_q(s, c)
                        if known == 0:
                            add_x(s, parity, c)
                if has_final(known) and known not in (NB - 1, NB):
                    normalise2(s)
                if has_ffn(known) and known != NB - 1:
                    hidden(s, 0)
                if has_proj(known):
                    stats_r(s, known)
                if has_ffn(known):
                    hidden(s, 2)
                if has_proj(known):
                    normalise1(s, known, parity, (0, 1))
                if has_ffn(known):
                    hidden(s, 3)
                if has_proj(known):
                    normalise1(s, known, parity, (2, 3))
                if has_norm(known):
                    for c in range(C):
                        normalise_x(s, parity, c)
                if known == NB - 1:
                    normalise2(s)
                if has_ffn(known):
                    hidden(s, 4)
                if has_norm(known):
                    split_xn(s, parity)
                if has_ffn(known):
                    hidden(s, HC - 1)
                if known == NB - 1:
                    split_h(s, HC - 1)
                if has_proj(known):
                    normalise_fm(s)

            dve.wait_ge(s_gamma, 16)
            nc.vector.tensor_scalar_mul(gamma_root[:, :], gamma_sb[:, :], ROOT_D).then_inc(s_gamma_root, 1)
            floor_norm(-2)
            dve.wait_ge(s_gamma_root, 1)
            for c in range(C):
                normalise_x(-2, 0, c, first=True)
            for c in range(C):
                split_xn(-2, 0, (c,))
                qkva_lo_part(c)
            floor_norm(-1)
            int_lo(0, gate_lo, gate_i, gate_hi, s_gate_lo, slice(0, C))
            scan(-1, 0)
            for c in range(C):
                normalise_x(-1, 1, c, first=True)
            split_xn(-1, 1)
            scan(-1, 1)
            for c in range(C):
                times_q(-1, c)
                add_x(-1, 1, c)
            int_lo(2, down_lo, down_i, down_hi, s_down_lo, slice(0, HC // 2))
            stats_r(-1, -1)
            int_lo(2, down_lo, down_i, down_hi, s_down_lo, slice(HC // 2, HC))
            normalise1(-1, -1, 1, range(TT))
            dve.wait_ge(s_lo_sums, 3)
            nc.vector.reduce_sum(lo_any[:, :], lo_sums[:, :], mybir.AxisListType.X).then_inc(s_lo_any0, 1)
            dve.wait_ge(s_lo_any0, 1)
            nc.vector.tensor_scalar_min(lo_any[:, :], lo_any[:, :], 1.0).then_inc(s_lo_any, 1)
            dve.wait_ge(s_lo_count, 1)
            nc.vector.tensor_scalar_min(lo_flag[:, :], ps[0:1, NPROJ - 1, 0:1], 1.0).then_inc(s_lo_flag, 1)
            scan(0, 0)
            for c in range(C):
                split_x1(0, -1, c)
            run_steps(dve, step)

        @block.gpsimd
        def _(pool):
            pool.memset(ident[:, :], 0.0).then_inc(s_ident0, 1)
            pool.memset(minus_half[:, :], -0.5).then_inc(s_ident0, 1)
            pool.wait_ge(s_ident0, 2)
            pool.affine_select(out=ident[:, :], in_=ident[:, :], compare_op=ALU.not_equal, fill=1.0,
                               base=0, pattern=[[-1, P]], channel_multiplier=1).then_inc(s_ident, 1)
            pool.memset(ones[:, :], 1.0).then_inc(s_const, 1)

            def inverse_std(var, s_var, rstd, s_rstd, n, tiles=slice(0, TT)):
                pool.wait_ge(s_var, n)
                nc.gpsimd.tensor_tensor(out=rstd[:, tiles], in0=var[:, tiles], in1=minus_half[:, tiles], op=ALU.pow)\
                    .then_inc(s_rstd, 1)

            def inverse_norm(s):
                if not isinstance(s, int) or s >= 1:
                    pool.wait_ge(s_norms_out, 16 * s)
                if isinstance(s, int) and s in (-1, 0):
                    pool.wait_ge(s_first_norms, s + 2)
                pool.wait_ge(s_floor, s + 3)
                nc.gpsimd.tensor_tensor(out=inv_norm[:, :], in0=sum_sq_floor[:, :], in1=minus_half[:, :],
                                        op=ALU.pow).then_inc(s_inv_norm, 1)

            def residual1(s, parity, c):
                pool.wait_ge(s_qy, C * (s + 1) + c + 1)
                nc.gpsimd.tensor_tensor(out=r_fm[:, c, :], in0=y[:, c, :], in1=xf_in[:, (parity + 1) % 2, c, :],
                                        op=ALU.add).then_inc(s_r_fm, 1)

            def split_h(s, p):
                pool.wait_ge(s_h_hi, HC * s + p + 1)
                nc.gpsimd.tensor_tensor(out=h_lo[:, p, :], in0=h[:, p % 2, :], in1=wide(h_hi[:, p, :]),
                                        op=ALU.subtract).then_inc(s_h_lo, 1)

            def step(s, known, parity):
                if known == NB:
                    for k in range(2):
                        inverse_std(var2, s_var2, rstd2, s_rstd2, NB + k, slice(2 * k, 2 * k + 2))
                elif has_final(known) and known != NB - 1:
                    inverse_std(var2, s_var2, rstd2, s_rstd2, s)
                if has_proj(known) and known != 0:
                    residual1(s, parity, 0)
                    residual1(s, parity, 1)
                if has_norm(known):
                    inverse_norm(s)
                if has_ffn(known):
                    split_h(s, 0)
                if has_proj(known):
                    inverse_std(var1, s_var1, mv1[:, 1, :], s_rstd1, s + 2)
                if has_ffn(known):
                    split_h(s, 1)
                    if known == NB - 1:
                        inverse_std(var2, s_var2, rstd2, s_rstd2, s)
                    for p in range(2, HC - 1 if known == NB - 1 else HC):
                        split_h(s, p)
            inverse_norm(-2)
            inverse_norm(-1)
            pool.wait_ge(s_up_f, 1)
            nc.gpsimd.tensor_tensor(out=up_lo[:, :, :], in0=wide(up_i[:, :, :]), in1=wide(up_hi[:, :, :]),
                                    op=ALU.subtract).then_inc(s_up_lo, 1)
            inverse_std(var1, s_var1, mv1[:, 1, :], s_rstd1, 1)
            run_steps(pool, step)


def kernel(L0_attn_x, L0_attn_W_qkva, L0_attn_gamma, L0_ffn_w_gate, L0_ffn_w_up, L0_ffn_w_down):
    import numpy as np
    import concourse.bacc as bacc
    from concourse.bass_utils import run_bass_kernel_spmd

    P = 128
    x = np.asarray(L0_attn_x)
    nb, n, d = x.shape

    def by_partition(w):
        w = np.asarray(w)
        return np.ascontiguousarray(w.T.reshape(-1, P, w.shape[0]).transpose(1, 0, 2))

    arrays = {
        "x_rows": np.ascontiguousarray(x.reshape(nb, P, n // P, d)),
        "x_fm": np.ascontiguousarray(x.transpose(0, 2, 1).reshape(nb, d // P, P, n).transpose(0, 2, 1, 3)),
        "w_qkva": by_partition(L0_attn_W_qkva),
        "gamma": np.ascontiguousarray(np.asarray(L0_attn_gamma).reshape(d // P, P).T),
        "w_gate": by_partition(L0_ffn_w_gate),
        "w_up": by_partition(L0_ffn_w_up),
        "w_down": by_partition(L0_ffn_w_down),
    }
    nc = bacc.Bacc("TRN2", target_bir_lowering=False, num_devices=1)
    args = [nc.dram_tensor(name, a.shape, mybir.dt.from_np(a.dtype), kind="ExternalInput").ap()
            for name, a in arrays.items()]
    out = nc.dram_tensor("out", arrays["x_rows"].shape, mybir.dt.float32, kind="ExternalOutput").ap()
    norms = nc.dram_tensor("norms", (2, P, n // P), mybir.dt.float32, kind="Internal").ap()
    stats = nc.dram_tensor("stats", (2, 2 * n // P, P), mybir.dt.float32, kind="Internal").ap()
    post_norm_scan_ffn(nc, *args, norms, stats, out)
    r = run_bass_kernel_spmd(nc, [arrays], core_ids=[0])
    got = np.asarray(r.results[0]["out"])
    return np.ascontiguousarray(got.transpose(0, 2, 1, 3).reshape(nb, n, d))
```
